# Optimizing a Trainium2 kernel written in Bass

```python
import numpy as np
import jax
import jax.numpy as jnp

def _softmax(x, axis=-1):
    return jax.nn.softmax(x, axis=axis)

def _gelu(x):
    return jax.nn.gelu(x, approximate=True)

def _silu(x):
    return jax.nn.silu(x)

def _sigmoid(x):
    return jax.nn.sigmoid(x)

def _layernorm(x, axis=-1, eps=1e-05):
    m = jnp.mean(x, axis=axis, keepdims=True)
    v = jnp.var(x, axis=axis, keepdims=True)
    return (x - m) / jnp.sqrt(v + eps)

def _scatter_add(tgt, idx, src, axis=0):
    return tgt.at[idx].add(src)

def _segment_sum(src, seg, n):
    return jax.ops.segment_sum(src, seg, n)
kernel_name = 'mk_seq_postln_d1_jaxref_r4_3b8f8a'

def setup_inputs(seed: int=0):
    np.random.seed(seed)
    _w = jnp.asarray

    def _L0_attn_setup():
        import math
        import jax
        import jax.numpy as jnp
        import numpy as np
        from jax import lax
        B_, L, D_MODEL = (2, 256, 512)
        D_STATE, D_CONV, EXPAND = (16, 4, 2)
        D_INNER = EXPAND * D_MODEL
        DT_RANK = math.ceil(D_MODEL / 16)

        def _silu(v):
            return v * jax.nn.sigmoid(v)

        def _mamba_forward(hidden_states, in_proj_w, conv_w, conv_b, x_proj_w, dt_proj_w, dt_proj_b, A_log, D, out_proj_w):
            b, l, _ = hidden_states.shape
            xz = jnp.einsum('bld,ed->bel', hidden_states, in_proj_w)
            x, z = (xz[:, :D_INNER, :], xz[:, D_INNER:, :])
            A = -jnp.exp(A_log.astype(jnp.float32))
            xp = jnp.pad(x, ((0, 0), (0, 0), (D_CONV - 1, 0)))
            x = lax.conv_general_dilated(xp, conv_w[:, None, :], window_strides=(1,), padding='VALID', dimension_numbers=('NCH', 'OIH', 'NCH'), feature_group_count=D_INNER)
            x = _silu(x + conv_b[None, :, None])
            x_dbl = jnp.einsum('bdl,kd->blk', x, x_proj_w)
            dt_lo = x_dbl[..., :DT_RANK]
            Bmat = x_dbl[..., DT_RANK:DT_RANK + D_STATE]
            Cmat = x_dbl[..., DT_RANK + D_STATE:]
            delta = jax.nn.softplus(jnp.einsum('blr,dr->bld', dt_lo, dt_proj_w) + dt_proj_b.astype(jnp.float32))
            xt = jnp.transpose(x, (2, 0, 1))
            dl = jnp.transpose(delta, (1, 0, 2))
            Bl = jnp.transpose(Bmat, (1, 0, 2))
            Cl = jnp.transpose(Cmat, (1, 0, 2))

            def step(h, inp):
                d_t, B_t, C_t, x_t = inp
                dA = jnp.exp(d_t[..., None] * A)
                h = h * dA + d_t[..., None] * B_t[:, None, :] * x_t[..., None]
                y_t = jnp.sum(h * C_t[:, None, :], axis=-1)
                return (h, y_t)
            h0 = jnp.zeros((b, D_INNER, D_STATE), jnp.float32)
            _, ys = lax.scan(step, h0, (dl, Bl, Cl, xt))
            y = jnp.transpose(ys, (1, 0, 2))
            y = y + jnp.transpose(x, (0, 2, 1)) * D[None, None, :]
            y = y * _silu(jnp.transpose(z, (0, 2, 1)))
            out = jnp.einsum('bld,ed->ble', y, out_proj_w)
            return out
        key = jax.random.key(seed)
        ks = jax.random.split(key, 8)
        hidden_states = jax.random.normal(ks[0], (B_, L, D_MODEL), jnp.float32)
        in_proj_w = jax.random.normal(ks[1], (2 * D_INNER, D_MODEL), jnp.float32) * D_MODEL ** (-0.5)
        conv_w = jax.random.normal(ks[2], (D_INNER, D_CONV), jnp.float32) * D_CONV ** (-0.5)
        conv_b = jnp.zeros((D_INNER,), jnp.float32)
        x_proj_w = jax.random.normal(ks[3], (DT_RANK + 2 * D_STATE, D_INNER), jnp.float32) * D_INNER ** (-0.5)
        dt_std = DT_RANK ** (-0.5)
        dt_proj_w = jax.random.uniform(ks[4], (D_INNER, DT_RANK), jnp.float32, minval=-dt_std, maxval=dt_std)
        dt = jnp.exp(jax.random.uniform(ks[5], (D_INNER,), jnp.float32) * (math.log(0.1) - math.log(0.001)) + math.log(0.001))
        dt = jnp.clip(dt, 0.0001)
        dt_proj_b = dt + jnp.log(-jnp.expm1(-dt))
        A_log = jnp.log(jnp.broadcast_to(jnp.arange(1, D_STATE + 1, dtype=jnp.float32), (D_INNER, D_STATE)))
        D = jnp.ones((D_INNER,), jnp.float32)
        out_proj_w = jax.random.normal(ks[6], (D_MODEL, D_INNER), jnp.float32) * D_INNER ** (-0.5)
        return {'hidden_states': hidden_states, 'in_proj_w': in_proj_w, 'conv_w': conv_w, 'conv_b': conv_b, 'x_proj_w': x_proj_w, 'dt_proj_w': dt_proj_w, 'dt_proj_b': dt_proj_b, 'A_log': A_log, 'D': D, 'out_proj_w': out_proj_w}
    _L0_attn_in = _L0_attn_setup()

    def _L0_ffn_setup():
        import jax, jax.numpy as jnp
        import numpy as np
        NUM_EXPERTS_PER_TOK = 2
        key = jax.random.key(seed)
        k1, k2, k3, k4 = jax.random.split(key, 4)
        B, S, D, O, E = (4, 512, 512, 512, 8)
        x = jax.random.normal(k1, (B, S, D), dtype=jnp.float32)
        gate_w = jax.random.normal(k2, (E, D), dtype=jnp.float32) * (1.0 / np.sqrt(D))
        expert_w = jax.random.normal(k3, (E, O, D), dtype=jnp.float32) * (1.0 / np.sqrt(D))
        expert_b = jax.random.normal(k4, (E, O), dtype=jnp.float32) * 0.01
        return {'x': x, 'gate_w': gate_w, 'expert_w': expert_w, 'expert_b': expert_b}
    _L0_ffn_in = _L0_ffn_setup()
    _d = {'L0_attn_hidden_states': _L0_attn_in['hidden_states'], 'L0_attn_in_proj_w': _L0_attn_in['in_proj_w'], 'L0_attn_conv_w': _L0_attn_in['conv_w'], 'L0_attn_conv_b': _L0_attn_in['conv_b'], 'L0_attn_x_proj_w': _L0_attn_in['x_proj_w'], 'L0_attn_dt_proj_w': _L0_attn_in['dt_proj_w'], 'L0_attn_dt_proj_b': _L0_attn_in['dt_proj_b'], 'L0_attn_A_log': _L0_attn_in['A_log'], 'L0_attn_D': _L0_attn_in['D'], 'L0_attn_out_proj_w': _L0_attn_in['out_proj_w'], 'L0_ffn_gate_w': _L0_ffn_in['gate_w'], 'L0_ffn_expert_w': _L0_ffn_in['expert_w'], 'L0_ffn_expert_b': _L0_ffn_in['expert_b']}
    _x0 = _d['L0_attn_hidden_states']
    _d['L0_attn_hidden_states'] = jax.random.normal(jax.random.fold_in(jax.random.key(seed), 1), (8, 512, 512), dtype=_x0.dtype)
    del _x0
    return _d

def reference(L0_attn_hidden_states, L0_attn_in_proj_w, L0_attn_conv_w, L0_attn_conv_b, L0_attn_x_proj_w, L0_attn_dt_proj_w, L0_attn_dt_proj_b, L0_attn_A_log, L0_attn_D, L0_attn_out_proj_w, L0_ffn_gate_w, L0_ffn_expert_w, L0_ffn_expert_b):

    def _L0_attn_ref(hidden_states, in_proj_w, conv_w, conv_b, x_proj_w, dt_proj_w, dt_proj_b, A_log, D, out_proj_w):
        import math
        import jax
        import jax.numpy as jnp
        import numpy as np
        from jax import lax
        B_, L, D_MODEL = (2, 256, 512)
        D_STATE, D_CONV, EXPAND = (16, 4, 2)
        D_INNER = EXPAND * D_MODEL
        DT_RANK = math.ceil(D_MODEL / 16)

        def _silu(v):
            return v * jax.nn.sigmoid(v)

        def _mamba_forward(hidden_states, in_proj_w, conv_w, conv_b, x_proj_w, dt_proj_w, dt_proj_b, A_log, D, out_proj_w):
            b, l, _ = hidden_states.shape
            xz = jnp.einsum('bld,ed->bel', hidden_states, in_proj_w)
            x, z = (xz[:, :D_INNER, :], xz[:, D_INNER:, :])
            A = -jnp.exp(A_log.astype(jnp.float32))
            xp = jnp.pad(x, ((0, 0), (0, 0), (D_CONV - 1, 0)))
            x = lax.conv_general_dilated(xp, conv_w[:, None, :], window_strides=(1,), padding='VALID', dimension_numbers=('NCH', 'OIH', 'NCH'), feature_group_count=D_INNER)
            x = _silu(x + conv_b[None, :, None])
            x_dbl = jnp.einsum('bdl,kd->blk', x, x_proj_w)
            dt_lo = x_dbl[..., :DT_RANK]
            Bmat = x_dbl[..., DT_RANK:DT_RANK + D_STATE]
            Cmat = x_dbl[..., DT_RANK + D_STATE:]
            delta = jax.nn.softplus(jnp.einsum('blr,dr->bld', dt_lo, dt_proj_w) + dt_proj_b.astype(jnp.float32))
            xt = jnp.transpose(x, (2, 0, 1))
            dl = jnp.transpose(delta, (1, 0, 2))
            Bl = jnp.transpose(Bmat, (1, 0, 2))
            Cl = jnp.transpose(Cmat, (1, 0, 2))

            def step(h, inp):
                d_t, B_t, C_t, x_t = inp
                dA = jnp.exp(d_t[..., None] * A)
                h = h * dA + d_t[..., None] * B_t[:, None, :] * x_t[..., None]
                y_t = jnp.sum(h * C_t[:, None, :], axis=-1)
                return (h, y_t)
            h0 = jnp.zeros((b, D_INNER, D_STATE), jnp.float32)
            _, ys = lax.scan(step, h0, (dl, Bl, Cl, xt))
            y = jnp.transpose(ys, (1, 0, 2))
            y = y + jnp.transpose(x, (0, 2, 1)) * D[None, None, :]
            y = y * _silu(jnp.transpose(z, (0, 2, 1)))
            out = jnp.einsum('bld,ed->ble', y, out_proj_w)
            return out
        return _mamba_forward(hidden_states, in_proj_w, conv_w, conv_b, x_proj_w, dt_proj_w, dt_proj_b, A_log, D, out_proj_w)

    def _L0_ffn_ref(x, gate_w, expert_w, expert_b):
        import jax, jax.numpy as jnp
        import numpy as np
        NUM_EXPERTS_PER_TOK = 2
        B, S, D = x.shape
        xf = x.reshape(B * S, D)
        gate_logits = xf @ gate_w.T
        top_vals, top_idx = jax.lax.top_k(gate_logits, NUM_EXPERTS_PER_TOK)
        w = jax.nn.softmax(top_vals.astype(jnp.float32), axis=-1).astype(x.dtype)
        y_all = jnp.einsum('td,eod->teo', xf, expert_w) + expert_b[None, :, :]
        y_sel = jnp.take_along_axis(y_all, top_idx[:, :, None], axis=1)
        out = jnp.sum(y_sel * w[:, :, None], axis=1)
        return out.reshape(B, S, -1)
    x = L0_attn_hidden_states
    x = _layernorm(x + _L0_attn_ref(x, L0_attn_in_proj_w, L0_attn_conv_w, L0_attn_conv_b, L0_attn_x_proj_w, L0_attn_dt_proj_w, L0_attn_dt_proj_b, L0_attn_A_log, L0_attn_D, L0_attn_out_proj_w), axis=-1)
    x = _layernorm(x + _L0_ffn_ref(x, L0_ffn_gate_w, L0_ffn_expert_w, L0_ffn_expert_b), axis=-1)
    return x

_drawn_inputs = setup_inputs


def setup_inputs(seed=0):
    import zlib

    import numpy as np

    out = dict(_drawn_inputs(seed))
    spreads = {'L0_attn_conv_b': (0.0, 0.1), 'L0_attn_D': (1.0, 0.2)}
    factors = {'L0_ffn_expert_b': 8.0}
    for name, (base, spread) in spreads.items():
        noise = np.random.default_rng([zlib.crc32(name.encode()), seed]).standard_normal(out[name].shape)
        drawn = base * np.exp(spread * noise) if base else spread * noise
        out[name] = jnp.asarray(drawn.astype(out[name].dtype))
    for name, factor in factors.items():
        out[name] = (out[name] * factor).astype(out[name].dtype)
    return out
```

```python
from contextlib import ExitStack

import concourse.bass as bass
from concourse import mybir

ALU = mybir.AluOpType
ACT = mybir.ActivationFunctionType
F32 = mybir.dt.float32
U32 = mybir.dt.uint32

P = 128
NB = 8
L = 512
DM = 512
DI = 2 * DM
NS = 16
RANK = DM // 16
TAPS = 4
NE = 8
KD = DM // P
ND = DI // P
NT = L // P
KX = RANK + 2 * NS
HALF = DI // DM
EPS = 1e-5
FORI = 3

USES_BANK = ("z", "yT", "out", "x1T", "gate", "wT", "bias", "moe", "x", "xproj", "Ct", "yinit", "dt")


def half_pieces(h):
    z, yt, out = ([(name, h, t) for t in range(NT)] for name in ("z", "yT", "out"))
    return [z[0], z[1], yt[0], z[2], yt[1], z[3], out[0], yt[2], out[1], yt[3], out[2], out[3]]


def moe_pieces(e):
    return [("moe", e, t) for t in range(NT)]


def each(name, n):
    return [(name, j) for j in range(n)]


EPI_HEAD = [("load_res",)] + half_pieces(0) + half_pieces(1)
X = each("x", ND)
X1T, BIAS, YINIT, DT = each("x1T", NT), each("bias", NT), each("yinit", ND), each("dt", ND)
TAIL = [("ln2",), ("ln2x",), ("store",)]

PRO = [("load_hidT",)] + X + [("xsilu",), ("xproj",), ("Ct",)] + YINIT
EPI = EPI_HEAD + [("ln1",), ("ln1x",)] + X1T + [("gate",), ("route",), ("wT",)] + BIAS \
    + sum([moe_pieces(e) for e in range(NE)], []) + TAIL
FULL = EPI_HEAD + [("load_hidT",), ("ln1",)] + X[0:2] + [("ln1x",), X[2]] + X1T + [X[3], ("gate",), X[4], ("route",), X[5]] \
    + [("wT",), X[6]] + BIAS + [X[7]] + moe_pieces(0) + [("xsilu",)] + moe_pieces(1) + [("xproj",)] + moe_pieces(2) + [("Ct",)] \
    + sum([[YINIT[2 * i], YINIT[2 * i + 1]] + moe_pieces(3 + i) for i in range(4)], []) + moe_pieces(7) + TAIL

STEPS = NS * NT
COST = {"z": 34, "x": 34, "out": 34, "moe": 34, "yT": 5, "x1T": 5, "yinit": 5, "xproj": 69, "bias": 9}


def spread(pieces, with_dt):
    first = 2
    total = sum(COST.get(x[0], 3) for x in pieces) or 1
    steps, done = [[] for _ in range(STEPS)], 0
    for x in pieces:
        steps[min(STEPS - 1, first + done * (STEPS - first) // total)].append(x)
        done += COST.get(x[0], 3)
    if with_dt:
        for q in range(NT):
            steps[STEPS - NT + q] = DT[2 * q:2 * q + 2] + steps[STEPS - NT + q]
    return steps


class Segment:

    def __init__(self, steps, blocks, next_blocks):
        self.steps = steps
        flat = [x for s in steps for x in s]
        self.use = {x: k for k, x in enumerate(x for x in flat if x[0] in USES_BANK)}
        self.blocks = blocks
        self.ahead = blocks[2:] + next_blocks


Z_O = [("Wz", 0), ("Wo", 0), ("Wz", 1), ("Wo", 1)]
W_X = [("Wx", 0), ("Wx", 1)]
W_E = [("We", e) for e in range(NE)]
SEG_FIRST = Segment([PRO + DT], W_X, W_X)
SEG_PRO = Segment(spread(PRO, True), W_X, Z_O[0:2])
SEG_FULL = Segment(spread(FULL, True), Z_O + W_X + W_E, Z_O[0:2])
SEG_EPI = Segment(spread(EPI, False), Z_O + W_E, Z_O[0:2])
SEG_LAST = Segment([EPI], Z_O + W_E, [])

PRO_USES, EPI_USES = len(SEG_PRO.use) // 2, len(SEG_EPI.use) // 2
PRO_W, EPI_W = len(W_X) // 2, len(Z_O + W_E) // 2
assert len(SEG_FULL.use) == 2 * (PRO_USES + EPI_USES)


def block_of(piece):
    name = piece[0]
    if name == "z":
        return ("Wz", piece[1]), piece[2] == NT - 1
    if name == "out":
        return ("Wo", piece[1]), piece[2] == NT - 1
    if name == "moe":
        return ("We", piece[1]), piece[2] == NT - 1
    if name == "x":
        return ("Wx", piece[1] // 4), piece[1] % 4 == 3
    return None, False


class When:

    def __init__(self, seg, b, odd, e_half, p_half, bank_base, w_base):
        self.seg, self.b, self.odd = seg, b, odd
        self.e, self.p, self.e_half, self.p_half = b - 1, b + 1, e_half, p_half
        self.bank_base, self.w_base = bank_base, w_base

    def bank(self, piece):
        k = self.seg.use[piece]
        return k % 2, self.bank_base + k // 2 + 1


def periods(engine, period, last):
    period(When(SEG_FIRST, -1, 1, 0, 0, 0, 0))
    period(When(SEG_PRO, 0, 0, 0, 0, PRO_USES, PRO_W))
    per, per_w = PRO_USES + EPI_USES, PRO_W + EPI_W
    with engine.Fori(0, FORI) as i:
        for u in range(2):
            period(When(SEG_FULL, i * 2 + (1 + u), 1 - u, i, i + 1,
                        i * (2 * per) + (2 * PRO_USES + u * per), i * (2 * per_w) + (2 * PRO_W + u * per_w)))
    done = 2 * FORI
    period(When(SEG_EPI, NB - 1, 1, (NB - 2) // 2, 0, 2 * PRO_USES + done * per, 2 * PRO_W + done * per_w))
    last(When(SEG_LAST, NB, 0, (NB - 1) // 2, 0, 2 * PRO_USES + done * per + EPI_USES, 2 * PRO_W + done * per_w + EPI_W))


def build(nc, hid, hidT, w_inT, conv_w, conv_b, w_xT, w_dtT, dt_b, A_log, D, w_outT, gateT, w_expT, exp_b, ident_c, iota_c, out):
    with ExitStack() as ctx:
        def sb(name, shape, dt=F32):
            return ctx.enter_context(nc.sbuf_tensor(name, shape, dt))

        def sem(name):
            return ctx.enter_context(nc.semaphore(name))

        def pair(name):
            return [sem(f"{name}{s}") for s in range(2)]

        w_x = sb("w_x", [P, ND, KX])
        w_dt = sb("w_dt", [RANK, DI])
        expb = sb("expb", [NE, DM])
        gate = sb("gate", [P, KD, NE])
        ident = sb("ident", [P, P])
        iota = sb("iota", [P, NE])
        cw = sb("cw", [P, ND, TAPS])
        cb = sb("cb", [P, ND])
        dtb = sb("dtb", [P, ND])
        dskip = sb("dskip", [P, ND])
        negA = sb("negA", [P, ND, NS])
        eps = sb("eps", [P, 1])
        wslot = [sb(f"wslot{s}", [P, KD, DM]) for s in range(2)]
        hT = [sb(f"hidT{s}", [P, KD, L]) for s in range(2)]
        xpre = [sb(f"xpre{s}", [P, L + TAPS - 1]) for s in range(2)]
        xact = sb("xact", [P, ND, L])
        xdbl = sb("xdbl", [KX, L])
        xd = [sb(f"xd{s}", [P, L]) for s in range(2)]
        sp = [sb(f"sp{s}", [P, L]) for s in range(2)]
        delta = sb("delta", [P, ND, L])
        u = sb("u", [P, ND, L])
        Bbc = [sb(f"Bbc{s}", [P, L]) for s in range(2)]
        dbu = [sb(f"dbu{s}", [P, L]) for s in range(4)]
        hst = [sb(f"hst{s}", [P, ND, L]) for s in range(2)]
        Ct = [sb(f"Ct{s}", [P, NT, NS]) for s in range(2)]
        y = [sb(f"y{s}", [P, NT, DI]) for s in range(2)]
        zs = [sb(f"zs{s}", [P, DM]) for s in range(2)]
        tokT = sb("tokT", [P, KD, L])
        res = sb("res", [P, NT, DM])
        st = sb("st", [P, NT, 6])
        mv = sb("mv", [P, NT, 2])
        lnv = sb("lnv", [P, NT])
        rstd = sb("rstd", [P, NT])
        lg = sb("lg", [P, NT, NE])
        mx = sb("mx", [P, NT, 8])
        mi = sb("mi", [P, NT, 8], U32)
        pick = sb("pick", [P, NT, 2])
        gap = sb("gap", [P, NT])
        eg = sb("eg", [P, NT])
        den = sb("den", [P, NT])
        w1 = sb("w1", [P, NT])
        w2 = sb("w2", [P, NT])
        m1 = sb("m1", [P, NT, NE])
        m2 = sb("m2", [P, NT, NE])
        wt = sb("wt", [P, NT, NE])
        wTs = sb("wTs", [NE, L])
        dA = [ctx.enter_context(nc.psum_tensor(f"dA{s}", [P, L], F32)) for s in range(2)]
        hTp = [ctx.enter_context(nc.psum_tensor(f"hTp{s}", [P, DI], F32)) for s in range(2)]
        bank = [ctx.enter_context(nc.psum_tensor(f"bank{s}", [P, 512], F32)) for s in range(2)]
        b_dram = nc.dram_tensor("b_scratch", (NB, NS, L), F32).ap()

        const_in = sem("const_in")
        negA_ready = sem("negA_ready")
        pads_ready = sem("pads_ready")
        w_loaded = pair("w_loaded")
        hidT_in = pair("hidT_in")
        res_in = sem("res_in")
        bank_full = pair("bank_full")
        bank_taken = pair("bank_taken")
        tap_done = sem("tap_done")
        conv_done = sem("conv_done")
        x_ready = sem("x_ready")
        xd_ready = sem("xd_ready")
        b_stored = sem("b_stored")
        b_loaded = pair("b_loaded")
        sp_step = sem("sp_step")
        sp_ready = sem("sp_ready")
        delta_ready = sem("delta_ready")
        u_ready = sem("u_ready")
        exp_done = sem("exp_done")
        dbu_done = sem("dbu_done")
        scan_done = sem("scan_done")
        hT_done = sem("hT_done")
        acc_done = sem("acc_done")
        yg_done = sem("yg_done")
        st_done = sem("st_done")
        mv_ready = sem("mv_ready")
        lnv_ready = sem("lnv_ready")
        rstd_ready = sem("rstd_ready")
        x1_ready = sem("x1_ready")
        route_step = sem("route_step")
        gap_ready = sem("gap_ready")
        eg_ready = sem("eg_ready")
        wt_ready = sem("wt_ready")
        out_ready = sem("out_ready")
        out_stored = sem("out_stored")
        seen = sem("seen")

        def tok(t):
            return slice(t * P, (t + 1) * P)

        def block_src(block):
            kind, h = block
            cols = slice(h * DM, (h + 1) * DM)
            if kind == "Wx":
                src = w_inT[:, cols]
            elif kind == "Wz":
                src = w_inT[:, DI + h * DM:DI + (h + 1) * DM]
            elif kind == "Wo":
                src = w_outT[cols, :]
            else:
                src = w_expT[:, cols]
            return src.rearrange("(k p) n -> p k n", p=P)

        NCONST = 12
        blk = ctx.enter_context(nc.Block())

        @blk.sync
        def _(sync):
            for dst, src in ((w_x[:, :, :], w_xT.rearrange("(k p) n -> p k n", p=P)), (w_dt[:, :], w_dtT), (expb[:, :], exp_b),
                             (gate[:, :, :], gateT.rearrange("(k p) n -> p k n", p=P)), (ident[:, :], ident_c), (iota[:, :], iota_c),
                             (cw[:, :, :], conv_w.rearrange("(k p) n -> p k n", p=P)),
                             (cb[:, :], conv_b.rearrange("(k p) -> p k", p=P)), (dtb[:, :], dt_b.rearrange("(k p) -> p k", p=P)),
                             (dskip[:, :], D.rearrange("(k p) -> p k", p=P)),
                             (negA[:, :, :], A_log.rearrange("(k p) n -> p k n", p=P))):
                with nc.allow_non_contiguous_dma(reason="small constants"):
                    sync.dma_start(dst, src).then_inc(const_in, 16)
            for s in range(2):
                sync.dma_start(wslot[s][:, :, :], block_src(W_X[s])).then_inc(w_loaded[s], 16)

            def load_B(w, n):
                if n == 0:
                    sync.wait_ge(b_stored, w.b * 16 + 16)
                sync.dma_start(Bbc[n % 2][:, :], b_dram[w.b, n:n + 1, :].broadcast_to((P, L))).then_inc(b_loaded[n % 2], 16)

            def piece(w, x):
                name, used_up = x[0], block_of(x)
                if name == "load_hidT":
                    slot = 1 - w.odd
                    if w.seg is SEG_FULL:
                        s, v = w.bank(("z", 1, NT - 1))
                        sync.wait_ge(bank_full[s], v)
                    sync.dma_start(hT[slot][:, :, :], hidT[w.p].rearrange("(k p) t -> p k t", p=P)).then_inc(hidT_in[slot], 16)
                elif name == "load_res":
                    if not (isinstance(w.e, int) and w.e == 0):
                        sync.wait_ge(out_stored, w.e * (16 * NT))
                    sync.dma_start(res[:, :, :], hid[w.e].rearrange("(t p) c -> p t c", p=P)).then_inc(res_in, 16)
                elif name == "xproj":
                    s, v = w.bank(x)
                    sync.wait_ge(bank_taken[s], v)
                    sync.dma_start(b_dram[w.p], xdbl[RANK:RANK + NS, :]).then_inc(b_stored, 16)
                elif name == "store":
                    for t in range(NT):
                        sync.wait_ge(out_ready, w.e * NT + (t + 1))
                        sync.dma_start(out[w.e, tok(t), :], res[:, t, :]).then_inc(out_stored, 16)
                elif used_up[1]:
                    k = w.seg.blocks.index(used_up[0])
                    if k < len(w.seg.ahead):
                        s, v = w.bank(x)
                        sync.wait_ge(bank_full[s], v)
                        sync.dma_start(wslot[k % 2][:, :, :], block_src(w.seg.ahead[k])).then_inc(w_loaded[k % 2], 16)

            def period(w):
                if w.seg is not SEG_FIRST:
                    for n in range(2):
                        if w.seg is not SEG_PRO:
                            sync.wait_ge(dbu_done, w.b * (NS * ND) + (n - 1) * ND)
                        load_B(w, n)
                for step, pieces in enumerate(w.seg.steps):
                    n, q = step // NT, step % NT
                    if w.seg is not SEG_FIRST and q == 0 and 1 <= n < NS - 1:
                        sync.wait_ge(dbu_done, w.b * (NS * ND) + n * ND)
                        load_B(w, n + 1)
                    for x in pieces:
                        piece(w, x)

            periods(sync, period, lambda w: [piece(w, x) for x in EPI])
            sync.wait_ge(out_stored, 16 * NT * NB)

        @blk.tensor
        def _(pe):
            def accumulate(dst, lhs, rhs, n):
                for k in range(n):
                    mm = nc.tensor.matmul(dst, lhs(k), rhs(k), start=(k == 0), stop=(k == n - 1))
                return mm

            def states(G, n, t, first):
                s = t % 2
                if t == 0:
                    pe.wait_ge(scan_done, G * ND + ND)
                if not (first and n == 0 and t < 2):
                    pe.wait_ge(acc_done, G * NT + (t - 1))
                for j in range(ND):
                    mm = nc.tensor.transpose(hTp[s][:, j * P:(j + 1) * P], hst[n % 2][:, j, tok(t)], ident[:, :])
                mm.then_inc(hT_done, 1)

            def piece(w, x):
                name = x[0]
                if name not in USES_BANK:
                    return
                s, v = w.bank(x)
                ps = bank[s]
                if not (isinstance(v, int) and v == 1):
                    pe.wait_ge(bank_taken[s], v - 1)
                block, used_up = block_of(x)
                if block:
                    k = w.seg.blocks.index(block)
                    W = wslot[k % 2]
                    pe.wait_ge(w_loaded[k % 2], w.w_base * 16 + 16 * (k // 2 + 1))
                if name == "x":
                    j, slot = x[1], 1 - w.odd
                    if j == 0:
                        pe.wait_ge(hidT_in[slot], w.p_half * 16 + 16)
                    mm = accumulate(ps[:, :], lambda k: W[:, k, tok(j % 4)], lambda k: hT[slot][:, k, :], KD)
                elif name == "xproj":
                    pe.wait_ge(x_ready, w.p * ND + ND)
                    mm = accumulate(ps[0:KX, :], lambda k: w_x[:, k, :], lambda k: xact[:, k, :], ND)
                elif name == "Ct":
                    sx, vx = w.bank(("xproj",))
                    pe.wait_ge(bank_taken[sx], vx)
                    for t in range(NT):
                        mm = nc.tensor.matmul(ps[:, t * NS:(t + 1) * NS], xdbl[0:KX, tok(t)], ident[0:KX, RANK + NS:KX], start=True, stop=True)
                elif name == "yinit":
                    j = x[1]
                    pe.wait_ge(xd_ready, w.p * ND + (j + 1))
                    for t in range(NT):
                        mm = nc.tensor.transpose(ps[:, tok(t)], xd[j % 2][:, tok(t)], ident[:, :])
                elif name == "dt":
                    j = x[1]
                    mm = nc.tensor.matmul(ps[:, :], w_dt[0:RANK, j * P:(j + 1) * P], xdbl[0:RANK, :], start=True, stop=True)
                elif name == "z":
                    slot, t = 1 - w.odd, x[2]
                    if x[1] == 0 and t == 0:
                        pe.wait_ge(hidT_in[slot], w.e_half * 16 + 16)
                    mm = accumulate(ps[:, :], lambda k: hT[slot][:, k, tok(t)], lambda k: W[:, k, :], KD)
                elif name == "yT":
                    h, t = x[1], x[2]
                    pe.wait_ge(yg_done, w.e * (HALF * NT) + (h * NT + t + 1))
                    for k in range(KD):
                        mm = nc.tensor.transpose(ps[:, tok(k)], zs[t % 2][:, tok(k)], ident[:, :])
                elif name == "out":
                    h, t = x[1], x[2]
                    sy, vy = w.bank(("yT", h, t))
                    pe.wait_ge(bank_taken[sy], vy)
                    mm = accumulate(ps[:, :], lambda k: tokT[:, k, tok(t)], lambda k: W[:, k, :], KD)
                elif name == "x1T":
                    t = x[1]
                    pe.wait_ge(x1_ready, w.e * NT + (t + 1))
                    for k in range(KD):
                        mm = nc.tensor.transpose(ps[:, tok(k)], res[:, t, tok(k)], ident[:, :])
                elif name == "gate":
                    for t in (NT - 2, NT - 1):
                        sy, vy = w.bank(("x1T", t))
                        pe.wait_ge(bank_taken[sy], vy)
                    for t in range(NT):
                        mm = accumulate(ps[:, t * NE:(t + 1) * NE], lambda k: tokT[:, k, tok(t)], lambda k: gate[:, k, :], KD)
                elif name == "wT":
                    pe.wait_ge(wt_ready, w.e + 1)
                    for t in range(NT):
                        mm = nc.tensor.matmul(ps[0:NE, tok(t)], wt[:, t, :], ident[:, :], start=True, stop=True)
                elif name == "bias":
                    t = x[1]
                    sy, vy = w.bank(("wT",))
                    pe.wait_ge(bank_taken[sy], vy)
                    mm = nc.tensor.matmul(ps[:, :], wTs[0:NE, tok(t)], expb[0:NE, :], start=True, stop=True)
                elif name == "moe":
                    t = x[2]
                    mm = accumulate(ps[:, :], lambda k: tokT[:, k, tok(t)], lambda k: W[:, k, :], KD)
                mm.then_inc(bank_full[s], 1)

            def period(w):
                first = isinstance(w.b, int) and w.b == 0
                for step, pieces in enumerate(w.seg.steps):
                    n, q = step // NT, step % NT
                    if w.seg is not SEG_FIRST:
                        if n == 0:
                            if not first and q < 2:
                                for t in (2 * q, 2 * q + 1):
                                    states(w.b * NS - 1, NS - 1, t, False)
                        else:
                            states(w.b * NS + (n - 1), n - 1, q, first)
                    for x in pieces:
                        piece(w, x)

            def last(w):
                for t in range(NT):
                    states(NB * NS - 1, NS - 1, t, False)
                for x in EPI:
                    piece(w, x)

            pe.wait_ge(const_in, 16 * (NCONST - 1))
            periods(pe, period, last)

        @blk.scalar
        def _(act):
            act.wait_ge(const_in, 16 * (NCONST - 1))
            nc.scalar.activation(negA[:, :, :], negA[:, :, :], ACT.Exp).then_inc(negA_ready, 1)
            act.wait_ge(negA_ready, 2)
            act.wait_ge(pads_ready, 3)

            def skip_term(w, j):
                act.wait_ge(x_ready, w.p * ND + (j + 1))
                nc.scalar.activation(xd[j % 2][:, :], xact[:, j, :], ACT.Copy, scale=dskip[:, j:j + 1]).then_inc(xd_ready, 1)

            def rsqrt(w, base):
                act.wait_ge(mv_ready, w.e * (2 * NT) + (base + 1) * NT)
                nc.scalar.activation(lnv[:, :], mv[:, :, 1], ACT.Ln, bias=eps[:, 0:1]).then_inc(lnv_ready, 1)
                act.wait_ge(lnv_ready, w.e * 2 + (base + 1))
                nc.scalar.activation(rstd[:, :], lnv[:, :], ACT.Exp, scale=-0.5).then_inc(rstd_ready, 1)

            def table(name):
                nc.scalar.preload_act_table_set(name)

            def piece(w, x):
                name = x[0]
                if name in ("z", "xsilu"):
                    table("silu_and_others")
                elif name in ("ln1", "ln2") or x == ("dt", 0):
                    table("natural_log_exp_and_others")
                if name in ("x", "xproj", "yinit", "dt", "z", "yT", "x1T", "wT"):
                    s, v = w.bank(x)
                    ps = bank[s]
                    act.wait_ge(bank_full[s], v)
                if name == "x":
                    j = x[1]
                    if not (isinstance(w.p, int) and w.p == 0 and j < 2):
                        act.wait_ge(conv_done, w.p * ND + (j - 1))
                    if not (isinstance(w.p, int) and w.p == 0):
                        act.wait_ge(u_ready, w.p * ND)
                    nc.scalar.activation(xact[:, j, :], ps[:, :], ACT.Identity, bias=cb[:, j:j + 1], scale=cw[:, j, TAPS - 1:TAPS])
                    nc.scalar.activation(xpre[j % 2][:, TAPS - 1:], ps[:, :], ACT.Copy).then_inc(bank_taken[s], 1)
                elif name == "xsilu":
                    for j in range(ND):
                        act.wait_ge(conv_done, w.p * ND + (j + 1))
                        nc.scalar.activation(xact[:, j, :], xact[:, j, :], ACT.Silu).then_inc(x_ready, 1)
                    table("exp_and_others")
                    for j in range(2):
                        skip_term(w, j)
                elif name == "xproj":
                    if not (isinstance(w.p, int) and w.p == 0):
                        act.wait_ge(b_stored, w.p * 16)
                    nc.scalar.activation(xdbl[:, :], ps[0:KX, :], ACT.Copy).then_inc(bank_taken[s], 1)
                elif name == "yinit":
                    j = x[1]
                    if w.seg is SEG_FULL:
                        act.wait_ge(yg_done, w.e * (HALF * NT) + HALF * NT)
                    nc.scalar.activation(y[1 - w.odd][:, :, j * P:(j + 1) * P], ps[:, :].rearrange("p (t d) -> p t d", t=NT),
                                         ACT.Copy).then_inc(bank_taken[s], 1)
                    if j + 2 < ND:
                        skip_term(w, j + 2)
                elif name == "dt":
                    j, a = x[1], sp[x[1] % 2]
                    if not (isinstance(w.p, int) and w.p == 0 and j < 2):
                        act.wait_ge(delta_ready, w.p * ND + (j - 1))
                    nc.scalar.activation(a[:, :], ps[:, :], ACT.Abs, bias=dtb[:, j:j + 1]).then_inc(sp_step, 1)
                    if w.seg is not SEG_FIRST:
                        act.wait_ge(exp_done, w.b * (NS * ND) + ((NS - 1) * ND + j + 1))
                    nc.scalar.activation(delta[:, j, :], ps[:, :], ACT.Relu, bias=dtb[:, j:j + 1]).then_inc(bank_taken[s], 1)
                    act.wait_ge(sp_step, w.p * (2 * ND) + (2 * j + 1))
                    nc.scalar.activation(a[:, :], a[:, :], ACT.Exp, scale=-1.0).then_inc(sp_step, 1)
                    act.wait_ge(sp_step, w.p * (2 * ND) + (2 * j + 2))
                    nc.scalar.activation(a[:, :], a[:, :], ACT.Ln, bias=1.0).then_inc(sp_ready, 1)
                elif name == "z":
                    nc.scalar.activation(zs[x[2] % 2][:, :], ps[:, :], ACT.Silu).then_inc(bank_taken[s], 1)
                    table("exp_and_others")
                elif name in ("yT", "x1T"):
                    t = x[-1]
                    nc.scalar.activation(tokT[:, :, tok(t)], ps[:, :].rearrange("p (k t) -> p k t", k=KD), ACT.Copy).then_inc(bank_taken[s], 1)
                elif name == "ln1":
                    rsqrt(w, 0)
                elif name == "ln2":
                    rsqrt(w, 1)
                elif name == "gate":
                    act.wait_ge(gap_ready, w.e + 1)
                    nc.scalar.activation(eg[:, :], gap[:, :], ACT.Exp).then_inc(eg_ready, 1)
                elif name == "wT":
                    nc.scalar.activation(wTs[:, :], ps[0:NE, :], ACT.Copy).then_inc(bank_taken[s], 1)

            def period(w):
                for step, pieces in enumerate(w.seg.steps):
                    n, q = step // NT, step % NT
                    if w.seg is not SEG_FIRST:
                        for j in (2 * q, 2 * q + 1):
                            if n == 0:
                                act.wait_ge(u_ready, w.b * ND + (j + 1))
                            if not (isinstance(w.b, int) and w.b == 0 and n == 0 and j < 2):
                                act.wait_ge(scan_done, w.b * (NS * ND) + (n * ND + j - 1))
                            nc.scalar.activation(dA[j % 2][:, :], delta[:, j, :], ACT.Exp, scale=negA[:, j, n:n + 1]).then_inc(exp_done, 1)
                    for x in pieces:
                        piece(w, x)

            periods(act, period, lambda w: [piece(w, x) for x in EPI])

        @blk.gpsimd
        def _(pool):
            def piece(w, x):
                if x[0] != "dt":
                    return
                j = x[1]
                pool.wait_ge(sp_ready, w.p * ND + (j + 1))
                nc.gpsimd.tensor_tensor(delta[:, j, :], delta[:, j, :], sp[j % 2][:, :], ALU.add).then_inc(delta_ready, 1)
                pool.wait_ge(delta_ready, w.p * ND + (j + 1))
                if w.seg is not SEG_FIRST:
                    pool.wait_ge(dbu_done, w.b * (NS * ND) + ((NS - 1) * ND + j + 1))
                nc.gpsimd.tensor_tensor(u[:, j, :], delta[:, j, :], xact[:, j, :], ALU.mult).then_inc(u_ready, 1)

            def period(w):
                for step, pieces in enumerate(w.seg.steps):
                    n, q = step // NT, step % NT
                    if w.seg is not SEG_FIRST:
                        if q == 0:
                            pool.wait_ge(b_loaded[n % 2], w.b * (16 * NS // 2) + 16 * (n // 2 + 1))
                        for j in (2 * q, 2 * q + 1):
                            if n == 0:
                                pool.wait_ge(u_ready, w.b * ND + (j + 1))
                            if not (isinstance(w.b, int) and w.b == 0 and n == 0 and j < 4):
                                pool.wait_ge(scan_done, w.b * (NS * ND) + (n * ND + j - 3))
                            nc.gpsimd.tensor_tensor(dbu[j % 4][:, :], u[:, j, :], Bbc[n % 2][:, :], ALU.mult).then_inc(dbu_done, 1)
                    for x in pieces:
                        piece(w, x)

            periods(pool, period, lambda w: None)

        @blk.vector
        def _(dve):
            for s in range(2):
                nc.vector.memset(xpre[s][:, 0:TAPS - 1], 0.0).then_inc(pads_ready, 1)
            nc.vector.memset(eps[:, :], EPS).then_inc(pads_ready, 1)
            dve.wait_ge(negA_ready, 1)
            nc.vector.tensor_scalar(negA[:, :, :], negA[:, :, :], -1.0, None, ALU.mult).then_inc(negA_ready, 1)

            def states(step, t, n, odd, first):
                if n == 0:
                    pass
                dve.wait_ge(hT_done, step * NT + (t + 1))
                if not (first and n == 0):
                    dve.wait_ge(acc_done, step * NT + (t + 1 - NT))
                nc.vector.scalar_tensor_tensor(y[odd][:, t, :], hTp[t % 2][:, :], Ct[odd][:, t, n:n + 1], y[odd][:, t, :],
                                               ALU.mult, ALU.add).then_inc(acc_done, 1)

            def norm(w, base, t):
                dve.wait_ge(rstd_ready, w.e * 2 + (base + 1))
                return nc.vector.tensor_scalar(res[:, t, :], res[:, t, :], mv[:, t, 0:1], rstd[:, t:t + 1], ALU.subtract, ALU.mult)

            def stats(w, base, t):
                nc.vector.bn_stats(st[:, t, :], res[:, t, :]).then_inc(st_done, 1)

            def aggregate(w, base):
                for t in range(NT):
                    dve.wait_ge(st_done, w.e * (2 * NT) + (base * NT + t + 1))
                    dve.sem_inc(seen, 1)
                    nc.vector.bn_aggr(mv[:, t, :], st[:, t, :]).then_inc(mv_ready, 1)

            def piece(w, x):
                name = x[0]
                if name in ("Ct", "out", "gate", "bias", "moe"):
                    s, v = w.bank(x)
                    ps = bank[s]
                    dve.wait_ge(bank_full[s], v)
                if name == "x":
                    j = x[1]
                    s, v = w.bank(x)
                    dve.wait_ge(bank_taken[s], v)
                    for k in range(TAPS - 1):
                        if k:
                            dve.wait_ge(tap_done, w.p * (2 * ND) + (2 * j + k))
                        tap = nc.vector.scalar_tensor_tensor(xact[:, j, :], xpre[j % 2][:, k:k + L], cw[:, j, k:k + 1], xact[:, j, :], ALU.mult, ALU.add)
                        tap.then_inc(conv_done if k == TAPS - 2 else tap_done, 1)
                elif name == "Ct":
                    nc.vector.tensor_copy(Ct[1 - w.odd][:, :, :], ps[:, 0:NT * NS].rearrange("p (t n) -> p t n", t=NT)).then_inc(bank_taken[s], 1)
                elif name == "z":
                    h, t = x[1], x[2]
                    s, v = w.bank(x)
                    dve.wait_ge(bank_taken[s], v)
                    if h == 0:
                        dve.wait_ge(acc_done, w.e * (NS * NT) + (NS - 1) * NT + t + 1)
                    nc.vector.tensor_tensor(zs[t % 2][:, :], zs[t % 2][:, :], y[1 - w.odd][:, t, h * DM:(h + 1) * DM], ALU.mult).then_inc(yg_done, 1)
                elif name == "out":
                    h, t = x[1], x[2]
                    if h == 0 and t == 0:
                        dve.wait_ge(res_in, w.e * 16 + 16)
                    if h:
                        so, vo = w.bank(("out", 0, t))
                        dve.wait_ge(bank_taken[so], vo)
                    nc.vector.tensor_tensor(res[:, t, :], ps[:, :], res[:, t, :], ALU.add).then_inc(bank_taken[s], 1)
                    if h:
                        dve.wait_ge(bank_taken[s], v)
                        stats(w, 0, t)
                elif name == "ln1":
                    aggregate(w, 0)
                elif name == "ln1x":
                    for t in range(NT):
                        norm(w, 0, t).then_inc(x1_ready, 1)
                elif name == "gate":
                    base = w.e * (3 * NT + 4)
                    nc.vector.tensor_copy(lg[:, :, :], ps[:, 0:NT * NE].rearrange("p (t e) -> p t e", t=NT)).then_inc(bank_taken[s], 1)
                    dve.wait_ge(bank_taken[s], v)
                    dve.sem_inc(seen, 1)
                    for t in range(NT):
                        nc.vector.max(mx[:, t, :], lg[:, t, :]).then_inc(route_step, 1)
                    for t in range(NT):
                        dve.wait_ge(route_step, base + (t + 1))
                        dve.sem_inc(seen, 1)
                        nc.vector.max_index(mi[:, t, :], mx[:, t, :], lg[:, t, :]).then_inc(route_step, 1)
                    nc.vector.tensor_tensor(gap[:, :], mx[:, :, 1], mx[:, :, 0], ALU.subtract).then_inc(gap_ready, 1)
                    dve.wait_ge(route_step, base + 2 * NT)
                    nc.vector.tensor_copy(pick[:, :, :], mi[:, :, 0:2]).then_inc(route_step, 1)
                elif name == "route":
                    base = w.e * (3 * NT + 4) + (2 * NT + 1)
                    dve.wait_ge(eg_ready, w.e + 1)
                    nc.vector.tensor_scalar(den[:, :], eg[:, :], 1.0, None, ALU.add).then_inc(route_step, 1)
                    dve.wait_ge(route_step, base + 1)
                    nc.vector.reciprocal(w1[:, :], den[:, :]).then_inc(route_step, 1)
                    dve.wait_ge(route_step, base + 2)
                    nc.vector.tensor_tensor(w2[:, :], eg[:, :], w1[:, :], ALU.mult).then_inc(route_step, 1)
                    dve.wait_ge(route_step, base + 3)
                    for t in range(NT):
                        nc.vector.tensor_scalar(m1[:, t, :], iota[:, :], pick[:, t, 0:1], w1[:, t:t + 1], ALU.is_equal, ALU.mult)
                        nc.vector.tensor_scalar(m2[:, t, :], iota[:, :], pick[:, t, 1:2], w2[:, t:t + 1], ALU.is_equal, ALU.mult).then_inc(route_step, 1)
                    dve.wait_ge(route_step, base + 3 + NT)
                    nc.vector.tensor_tensor(wt[:, :, :], m1[:, :, :], m2[:, :, :], ALU.add).then_inc(wt_ready, 1)
                elif name == "bias":
                    t = x[1]
                    dve.wait_ge(x1_ready, w.e * NT + (t + 1))
                    nc.vector.tensor_tensor(res[:, t, :], ps[:, :], res[:, t, :], ALU.add).then_inc(bank_taken[s], 1)
                elif name == "moe":
                    ex, t = x[1], x[2]
                    so, vo = w.bank(("moe", ex - 1, t) if ex else ("bias", t))
                    dve.wait_ge(bank_taken[so], vo)
                    nc.vector.scalar_tensor_tensor(res[:, t, :], ps[:, :], wt[:, t, ex:ex + 1], res[:, t, :], ALU.mult, ALU.add).then_inc(bank_taken[s], 1)
                    if ex == NE - 1:
                        dve.wait_ge(bank_taken[s], v)
                        stats(w, 1, t)
                elif name == "ln2":
                    aggregate(w, 1)
                elif name == "ln2x":
                    for t in range(NT):
                        norm(w, 1, t).then_inc(out_ready, 1)

            def period(w):
                first = isinstance(w.b, int) and w.b == 0
                for step, pieces in enumerate(w.seg.steps):
                    n, q = step // NT, step % NT
                    if w.seg is not SEG_FIRST:
                        for j in (2 * q, 2 * q + 1):
                            tile = n * ND + j + 1
                            dve.wait_ge(exp_done, w.b * (NS * ND) + tile)
                            dve.wait_ge(dbu_done, w.b * (NS * ND) + tile)
                            if not (first and n < 2):
                                dve.wait_ge(hT_done, w.b * (NS * NT) + (n - 1) * NT)
                            nc.vector.tensor_tensor_scan(hst[n % 2][:, j, :], dA[j % 2][:, :], dbu[j % 4][:, :], 0.0, ALU.mult, ALU.add).then_inc(scan_done, 1)
                        if n == 0:
                            if not first and q < 2:
                                for t in (2 * q, 2 * q + 1):
                                    states(w.b * NS - 1, t, NS - 1, 1 - w.odd, False)
                        else:
                            states(w.b * NS + (n - 1), q, n - 1, w.odd, first)
                    for x in pieces:
                        piece(w, x)

            def last(w):
                for t in range(NT):
                    states(NB * NS - 1, t, NS - 1, 1, False)
                for x in EPI:
                    piece(w, x)

            periods(dve, period, last)


def kernel(**inputs):
    import numpy as np
    import concourse.bacc as bacc
    from concourse.bass_utils import run_bass_kernel_spmd

    def arr(name):
        return np.asarray(inputs[name])

    hid = arr("L0_attn_hidden_states")
    arrays = {
        "hid": hid,
        "hidT": hid.transpose(0, 2, 1),
        "w_inT": arr("L0_attn_in_proj_w").T,
        "conv_w": arr("L0_attn_conv_w"),
        "conv_b": arr("L0_attn_conv_b"),
        "w_xT": arr("L0_attn_x_proj_w").T,
        "w_dtT": arr("L0_attn_dt_proj_w").T,
        "dt_b": arr("L0_attn_dt_proj_b"),
        "A_log": arr("L0_attn_A_log"),
        "D": arr("L0_attn_D"),
        "w_outT": arr("L0_attn_out_proj_w").T,
        "gateT": arr("L0_ffn_gate_w").T,
        "w_expT": arr("L0_ffn_expert_w").transpose(2, 0, 1).reshape(DM, NE * DM),
        "exp_b": arr("L0_ffn_expert_b"),
        "ident_c": np.eye(P, dtype=np.float32),
        "iota_c": np.tile(np.arange(NE, dtype=np.float32), (P, 1)),
    }
    arrays = {k: np.ascontiguousarray(v) for k, v in arrays.items()}
    nc = bacc.Bacc("TRN2", target_bir_lowering=False, num_devices=1)
    args = [nc.dram_tensor(f"in_{k}", v.shape, mybir.dt.from_np(v.dtype), kind="ExternalInput").ap() for k, v in arrays.items()]
    out = nc.dram_tensor("out", hid.shape, F32, kind="ExternalOutput").ap()
    build(nc, *args, out)
    r = run_bass_kernel_spmd(nc, [{f"in_{k}": v for k, v in arrays.items()}], core_ids=[0])
    return r.results[0]["out"]
```

```python
from contextlib import ExitStack

import concourse.bass as bass
from concourse import mybir

ALU = mybir.AluOpType
ACT = mybir.ActivationFunctionType
F32 = mybir.dt.float32
U32 = mybir.dt.uint32
I32 = mybir.dt.int32
AX = mybir.AxisListType

P = 128
NB = 8
L = 512
DM = 512
DI = 2 * DM
NS = 16
RANK = DM // 16
TAPS = 4
NE = 8
TOP = 2
KD = DM // P
ND = DI // P
NT = L // P
KX = RANK + 2 * NS
HALF = DI // DM
EPS = 1e-5
TILES = (TOP * L + NE * (P - 1)) // P
FORI = 3

USES_BANK = ("z", "yT", "out", "x1T", "gate", "count", "rank", "wT", "bias", "xsT", "moe", "x", "xproj", "Ct", "yinit", "dt")
QUARTERS = ND // 2
STEPS = NS * QUARTERS
NH = HALF * NT
BANKS = 3

Z_SLOTS = 4


def each(name, n):
    return [(name, j) for j in range(n)]


def by_half(name):
    return [(name, h, t) for h in range(HALF) for t in range(NT)]


EPI = [("load_res",)] + by_half("out") + by_half("yT") + by_half("z") + [("ln1",), ("ln1x",)] + each("x1T", NT) \
    + [("gate",), ("count",), ("rank",), ("place",)] + each("scatter", NT) + [("load_E",), ("route",), ("wT",)] + each("xsT", TILES) \
    + each("bias", NT) + each("moe", TILES) + each("gather", NT // 2)
END = each("gather", NT)[NT // 2:] + each("combine", NT) + [("ln2",), ("ln2x",), ("store",)]
PRO = [("load_hx",)] + each("x", ND) + each("sig", ND) + [("load_hz",)] + each("xproj", 2) + [("Ct",)] + each("skip", ND) + each("yinit", ND) + each("dt", ND)


def needs(x):
    name, k = x[0], x[-1] if len(x) == 2 else 0
    i = x[1] * NT + x[2] if len(x) == 3 else None

    def half(name, i):
        return (name, i // NT, i % NT)

    if name == "z":
        return [(half("yT", i - Z_SLOTS), 0), (half("z", i - 1), 2 if i == NT else 0), (("combine", NT - 1), 0)]
    if name == "yT":
        return [(half("z", i), 3), (half("out", i - 4), 0)]
    if name == "out":
        return [(half("yT", i), 2), (half("out", i - 1), 2 if i == NT else 0), (("load_res",), 1)]
    return {
        "ln1": [(half("out", HALF * NT - 1), 1)], "ln1x": [(("ln1",), 3)], "x1T": [(("ln1x",), 1 + (k > 1))], "gate": [(("x1T", NT - 1), 2)],
        "count": [(("gate",), 3)], "rank": [(("count",), 0)], "place": [(("rank",), 1)], "scatter": [(("place",), 2 + (k == NT - 1))],
        "load_E": [(("place",), 1)], "route": [(("place",), 1)], "wT": [(("route",), 1)],
        "bias": [(("wT",), 2), (("scatter", NT - 1), 3), (("bias", k - 1), 3)] if name == "bias" else [],
        "xsT": [(("scatter", NT - 1), 3), (("xsT", k - 2), 2), (("moe", k - 4), 0)] if name == "xsT" else [],
        "moe": [(("xsT", k), 2), (("moe", k - 2), 2)] if name == "moe" else [],
        "gather": [(("moe", TILES - 1), 3)] if k < NT // 2 else [], "combine": [(("combine", k - 2), 1)] if name == "combine" else [], "ln2": [(("combine", NT - 1), 0)],
        "ln2x": [(("ln2",), 2)], "store": [(("ln2x",), 0)],
        "load_res": [(("store",), 0)],
        "load_hx": [(half("z", HALF * NT - 1), 0)], "load_hz_e": [(half("z", HALF * NT - 1), 0)],
        "x": [(("load_hx",), 3), (("x", k - 1), 1), (("x", k - 2), 3)] if name == "x" else [],
        "sig": [(("x", k), 3)], "load_hz": [(("x", ND - 1), 0)], "xproj": [(("sig", ND - 1), 4)], "Ct": [(("xproj", 1), 2)],
        "yinit": [(("skip", k), 1)] if name == "yinit" else [],
        "skip": [(("sig", ND - 1), 4) if k < 3 else (("yinit", k - 3), 1)] if name == "skip" else [],
        "dt": [(("xproj", 1), 2), (("yinit", ND - 1), 1), (("dt", k - 1), 1), (("dt", k - 2), 3)] if name == "dt" else [],
    }.get(name, [])


SHARES = {"z": 4, "x": 4, "out": 4, "moe": 4, "xproj": 4}
COST = {"yT": 0.5, "x1T": 0.5, "xsT": 0.5, "yinit": 0.5, "gate": 3.0, "count": 0.1, "rank": 0.2, "Ct": 0.1}
ROOM = 4.4
LAG = {
    "act": {"sig": 0, "skip": 0, "gate": 2, "ln1": 2},
    "dve": {"x": 1, "z": 2, "ln1": 0, "ln1x": 0, "place": 0, "route": 0, "combine": 0, "ln2": 0, "ln2x": 0},
    "pool": {"sig": 2, "scatter": 0, "gather": 0, "dt": 4},
}
DEFAULT_LAG = {"sp": 0, "act": 1, "dve": 1, "pool": 1}


def plan(pieces):
    shares, through, waiting, users, over, at = [], {}, list(pieces), [], 0.0, 0

    def can_start(x):
        if x in users:
            return True
        if x[0] in USES_BANK and len(users) >= BANKS and through.get(users[-BANKS], at) >= at:
            return False
        return all(p not in pieces or (p in through and through[p] + d <= at) for p, d in needs(x))

    while waiting:
        room, row = ROOM + min(over, 0.0), []
        while room > 0:
            x = next((x for x in waiting if can_start(x)), None)
            if x is None:
                break
            waiting.remove(x)
            if x[0] in USES_BANK:
                begun = sum(y == x for r in shares for y, _ in r)
                users += [x] if not begun else []
                for share in range(begun, SHARES.get(x[0], 1)):
                    if room <= 0:
                        waiting.insert(0, x)
                        break
                    row.append((x, share))
                    room -= COST.get(x[0], 1.0)
                else:
                    through[x] = at
            else:
                through[x] = at
        over = room
        shares.append(row)
        at += 1
    return shares, through


class Segment:

    def __init__(self, pieces, blocks, next_blocks, steps=STEPS):
        self.shares, self.through = plan(pieces)
        self.steps = steps
        self.use = {x: k for k, x in enumerate(x for row in self.shares for x, share in row if share == 0)}
        self.blocks = blocks
        self.place = {x: (s, k) for s in range(2) for k, x in enumerate(blocks[s])}
        self.after = {x: (blocks[s] + next_blocks[s:s + 1])[k + 1:k + 2] for x, (s, k) in self.place.items()}

        self.rows = {engine: self.parts(engine) for engine in ("sp", "pe", "act", "pool", "dve")}

    def parts(self, engine):
        rows = [[] for _ in range(self.steps or 1)]
        if engine == "pe":
            parts = [(at, x) for at, row in enumerate(self.shares) for x in row]
        else:
            parts = sorted(((at + LAG.get(engine, {}).get(x[0], DEFAULT_LAG[engine]), x) for x, at in self.through.items()), key=lambda p: p[0])
        for at, x in parts:
            rows[min(len(rows) - 1, at)].append(x)
        return rows


def slots(*parts):
    return [sum([p[s] for p in parts], []) for s in range(2)]


W_ZO = [[("Wz", 0), ("Wz", 1)], [("Wo", 0), ("Wo", 1)]]
W_X = [[("Wx", 0)], [("Wx", 1)]]
W_E = [[("We", k) for k in range(1, TILES, 2)], [("We", k) for k in range(0, TILES, 2)]]
FIRST_X, FIRST_ZO = [("Wx", 0), ("Wx", 1)], [("Wz", 0), ("Wo", 0)]
FULL = END + EPI[:EPI.index(("xsT", 0))] + PRO + EPI[EPI.index(("xsT", 0)):]
SEG_FIRST = Segment([x for x in PRO if x[0] not in ("load_hx", "load_hz")], W_X, FIRST_X, 0)
SEG_PRO = Segment(PRO, W_X, FIRST_ZO)
SEG_FULL = Segment(FULL, slots(W_ZO, W_X, W_E), FIRST_ZO)
SEG_EPI = Segment(END + EPI + [("load_hz_e",)], slots(W_ZO, W_E), FIRST_ZO)
SEG_LAST = Segment(END + EPI, slots(W_ZO, W_E), [], 0)
SEG_END = Segment(END, [[], []], [], 0)
TURN = 8
assert all(SEG_FULL.rows[engine][:TURN] == SEG_EPI.rows[engine][:TURN] for engine in SEG_FULL.rows)
assert max(SEG_FULL.through[x] + 1 for x in END) < TURN

PRO_USES, EPI_USES = len(SEG_PRO.use) // BANKS, len(SEG_EPI.use) // BANKS
PRO_W, EPI_W = [len(x) for x in SEG_PRO.blocks], [len(x) for x in SEG_EPI.blocks]
assert len(SEG_PRO.use) == BANKS * PRO_USES and len(SEG_EPI.use) == BANKS * EPI_USES


def block_of(piece):
    name = piece[0]
    if name == "z":
        return ("Wz", piece[1]), piece[2] == NT - 1
    if name == "out":
        return ("Wo", piece[1]), piece[2] == NT - 1
    if name == "moe":
        return ("We", piece[1]), True
    if name == "x":
        return ("Wx", piece[1] // KD), piece[1] % KD == KD - 1
    return None, False


LAST_READER = {block_of(x)[0]: x for x in PRO + EPI if block_of(x)[1]}


class When:

    def __init__(self, seg, b, odd, bank_base, w_base, start=0, stop=STEPS, leave_out=()):
        self.seg, self.b, self.odd = seg, b, odd
        self.d, self.e, self.p = b - 2, b - 1, b + 1
        self.bank_base, self.w_base = bank_base, w_base
        self.span, self.leave_out = range(start, min(stop, seg.steps or 1)), leave_out

    def rows(self, engine):
        for step in self.span:
            yield step, [x for x in self.seg.rows[engine][step] if x not in self.leave_out]

    def bank(self, piece):
        k = self.seg.use[piece]
        return k % BANKS, self.bank_base + k // BANKS + 1

    def weights(self, block):
        s, k = self.seg.place[block]
        return s, self.w_base[s] + (k + 1)


def periods(engine, period, last, end):
    def w_base(pros, epis):
        return [pros * PRO_W[s] + epis * EPI_W[s] for s in range(2)]

    period(When(SEG_FIRST, -1, 1, 0, w_base(0, 0)))
    period(When(SEG_PRO, 0, 0, PRO_USES, w_base(1, 0)))

    def full(b, odd, before, **span):
        return When(SEG_FULL, b, odd, before * (PRO_USES + EPI_USES) + 2 * PRO_USES,
                    [before * (PRO_W[s] + EPI_W[s]) + 2 * PRO_W[s] for s in range(2)], **span)

    period(full(1, 1, 0, stop=TURN, leave_out=END))
    with engine.Fori(0, FORI) as i:
        for u in range(2):
            period(full(i * 2 + (1 + u), 1 - u, i * 2 + u, start=TURN))
            period(full(i * 2 + (2 + u), u, i * 2 + (1 + u), stop=TURN))
    done = 2 * FORI
    uses = 2 * PRO_USES + done * (PRO_USES + EPI_USES)
    period(When(SEG_EPI, NB - 1, 1, uses, w_base(NB, done), start=TURN))
    last(When(SEG_LAST, NB, 0, uses + EPI_USES, w_base(NB, done + 1)))
    end(When(SEG_END, NB + 1, 1, 0, [0, 0]))


def build(nc, hid, hidT, w_inT, conv_w, conv_b, w_xT, w_dtT, dt_b, A_log, D, w_outT, gateT, w_expT, exp_b, ident_c, before_c, ramp_c, out):
    with ExitStack() as ctx:
        def sb(name, shape, dt=F32):
            return ctx.enter_context(nc.sbuf_tensor(name, shape, dt))

        def sem(name):
            return ctx.enter_context(nc.semaphore(name))

        def pair(name):
            return [sem(f"{name}{s}") for s in range(2)]

        w_x = sb("w_x", [P, ND, KX])
        w_rows = sb("w_rows", [KX + NE, DI])
        w_dt, expb = w_rows[0:RANK, :], w_rows[KX:KX + NE, 0:DM]
        gate = sb("gate", [P, KD, NE])
        ident = sb("ident", [P, P])
        before = sb("before", [P, P])
        ones = sb("ones", [P, P])
        ramp = sb("ramp", [P, 2 * NE + NT])
        cw = sb("cw", [P, ND, TAPS])
        cb = sb("cb", [P, ND])
        dtb = sb("dtb", [P, ND])
        dskip = sb("dskip", [P, ND])
        negA = sb("negA", [P, ND, NS])
        eps = sb("eps", [P, 1])
        wslot = [sb(f"wslot{s}", [P, KD, DM]) for s in range(2)]
        hT = sb("hidT", [P, KD, L])
        xpre = [sb(f"xpre{s}", [P, L + TAPS - 1]) for s in range(2)]
        rows = sb("rows", [KX + NE, L])
        xdbl, wTs = rows[0:KX, :], rows[KX:KX + NE, :]
        side = [sb(f"side{s}", [P, L]) for s in range(2)]
        delta = [sb(f"delta{s}", [P, ND, L]) for s in range(2)]
        u = [sb(f"u{s}", [P, ND, L]) for s in range(2)]
        Bbc = [sb(f"Bbc{s}", [P, L]) for s in range(2)]
        dbu = [sb(f"dbu{s}", [P, L]) for s in range(4)]
        hst = [sb(f"hst{s}", [P, ND, L]) for s in range(2)]
        Ct = [sb(f"Ct{s}", [P, NT, NS]) for s in range(2)]
        y = [sb(f"y{s}", [P, NT, DI]) for s in range(2)]
        zs = [sb(f"zs{s}", [P, DM]) for s in range(2)]
        tokT = sb("tokT", [P, KD, L])
        res = sb("res", [P, NT, DM])
        st = sb("st", [P, NT, 6])
        mv = sb("mv", [P, NT, 2])
        lnv = sb("lnv", [P, NT])
        rstd = sb("rstd", [P, NT])
        lg = sb("lg", [P, NT, NE])
        mx = sb("mx", [P, NT, 8])
        mi = sb("mi", [P, NT, 8], U32)
        pick = sb("pick", [P, NT, TOP])
        hit = sb("hit", [P, NT, TOP, NE])
        hits = sb("hits", [P, NT, NE])
        gap = sb("gap", [P, NT])
        eg = sb("eg", [P, NT])
        den = sb("den", [P, NT])
        mix = sb("mix", [P, NT, TOP])
        hit_w = sb("hit_w", [P, NT, TOP, NE])
        wt = sb("wt", [P, NT, NE])
        over = sb("over", [P, NE, NT])
        tiles = sb("tiles", [P, NE])
        end = sb("end", [P, NE])
        begin = sb("begin", [P, NE])
        row = sb("row", [P, NT, NE])
        hit_row = sb("hit_row", [P, NT, TOP, NE])
        place = sb("place", [P, NT, TOP], U32)
        past = sb("past", [1, TILES, NE])
        owner = sb("owner", [1, TILES])
        tile_expert = sb("tile_expert", [1, TILES], I32)
        ysb = [sb("ysb", [P, DM])[:, :], xpre[1][:, TAPS - 1:]]
        third = [side[0][:, :], side[1][:, :], xpre[0][:, TAPS - 1:]]
        zy = [xpre[0][:, TAPS - 1:], xpre[1][:, TAPS - 1:], zs[0][:, :], zs[1][:, :]]
        dA = [ctx.enter_context(nc.psum_tensor(f"dA{s}", [P, L], F32)) for s in range(2)]
        hTp = [ctx.enter_context(nc.psum_tensor(f"hTp{s}", [P, DM], F32)) for s in range(3)]
        bank = [ctx.enter_context(nc.psum_tensor(f"bank{s}", [P, 512], F32)) for s in range(BANKS)]
        b_dram = nc.dram_tensor("b_scratch", (NB, NS, L), F32).ap()
        xs_dram = nc.dram_tensor("sorted_tokens", (TILES * P, DM), F32).ap()
        ys_dram = nc.dram_tensor("sorted_results", (TILES * P, DM), F32).ap()

        conv_in = sem("conv_in")
        const_in = sem("const_in")
        negA_ready = sem("negA_ready")
        pads_ready = sem("pads_ready")
        w_loaded = pair("w_loaded")
        hidT_in = sem("hidT_in")
        res_in = sem("res_in")
        bank_full = [sem(f"bank_full{s}") for s in range(BANKS)]
        bank_taken = [sem(f"bank_taken{s}") for s in range(BANKS)]
        tap_done = sem("tap_done")
        conv_done = sem("conv_done")
        sig_step = sem("sig_step")
        x_ready = sem("x_ready")
        xd_ready = sem("xd_ready")
        b_stored = sem("b_stored")
        b_loaded = pair("b_loaded")
        sp_step = sem("sp_step")
        sp_ready = sem("sp_ready")
        delta_ready = sem("delta_ready")
        u_ready = sem("u_ready")
        exp_done = sem("exp_done")
        dbu_done = sem("dbu_done")
        scan_done = sem("scan_done")
        hT_done = sem("hT_done")
        acc_done = sem("acc_done")
        zsig_step = sem("zsig_step")
        zy_done = sem("zy_done")
        yg_done = sem("yg_done")
        st_done = sem("st_done")
        mv_ready = sem("mv_ready")
        lnv_ready = sem("lnv_ready")
        rstd_ready = sem("rstd_ready")
        x1_ready = sem("x1_ready")
        route_step = sem("route_step")
        gap_ready = sem("gap_ready")
        eg_ready = sem("eg_ready")
        wt_ready = sem("wt_ready")
        hits_ready = sem("hits_ready")
        place_ready = sem("place_ready")
        owner_ready = sem("owner_ready")
        xs_zeroed = sem("xs_zeroed")
        scattered = sem("scattered")
        xs_in = pair("xs_in")
        ys_stored = pair("ys_stored")
        gathered = pair("gathered")
        combined = sem("combined")
        out_ready = sem("out_ready")
        out_stored = sem("out_stored")
        seen, seen_sp, seen_pool = sem("seen"), sem("seen_sp"), sem("seen_pool")

        def tok(t):
            return slice(t * P, (t + 1) * P)

        def block_src(block):
            kind, h = block
            cols = slice(h * DM, (h + 1) * DM)
            if kind == "Wx":
                src = w_inT[:, cols]
            elif kind == "Wz":
                src = w_inT[:, DI + h * DM:DI + (h + 1) * DM]
            elif kind == "Wo":
                src = w_outT[cols, :]
            else:
                src = w_expT[h]
            return src.rearrange("(k p) n -> p k n", p=P)

        NCONST = 10

        def tile_slot(k):
            return k % 2, k // 2 + 1, (TILES + 1 - k % 2) // 2

        def choices(t):
            return tokT[:, t, :], (zs[0][:, :], zs[1][:, :], ysb[0], xpre[0][:, TAPS - 1:])[t]

        blk = ctx.enter_context(nc.Block())

        @blk.sync
        def _(sync):
            sync.dma_start(hT[:, :, :], hidT[0].rearrange("(k p) t -> p k t", p=P)).then_inc(hidT_in, 16)
            sync.dma_start(wslot[0][:, :, :], block_src(FIRST_X[0])).then_inc(w_loaded[0], 16)
            with nc.allow_non_contiguous_dma(reason="small constants"):
                sync.dma_start(cw[:, :, :], conv_w.rearrange("(k p) n -> p k n", p=P)).then_inc(conv_in, 16)
                sync.dma_start(cb[:, :], conv_b.rearrange("(k p) -> p k", p=P)).then_inc(conv_in, 16)
            sync.dma_start(wslot[1][:, :, :], block_src(FIRST_X[1])).then_inc(w_loaded[1], 16)
            for dst, src in ((w_x[:, :, :], w_xT.rearrange("(k p) n -> p k n", p=P)), (ident[:, :], ident_c),
                             (negA[:, :, :], A_log.rearrange("(k p) n -> p k n", p=P)),
                             (dskip[:, :], D.rearrange("(k p) -> p k", p=P)), (w_dt, w_dtT), (dtb[:, :], dt_b.rearrange("(k p) -> p k", p=P)),
                             (gate[:, :, :], gateT.rearrange("(k p) n -> p k n", p=P)), (expb, exp_b), (before[:, :], before_c), (ramp[:, :], ramp_c)):
                with nc.allow_non_contiguous_dma(reason="small constants"):
                    sync.dma_start(dst, src).then_inc(const_in, 16)
            sync.sem_inc(out_stored, 1)

            def load_B(b, n):
                sync.dma_start(Bbc[n % 2][:, :], b_dram[b, n:n + 1, :].broadcast_to((P, L))).then_inc(b_loaded[n % 2], 16)

            def load_expert(w, k):
                sync.sem_inc(seen_sp, 1)
                e = sync.value_load(tile_expert[0:1, k:k + 1], min_val=0, max_val=NE - 1)
                s = w.weights(("We", k))[0]
                sync.dma_start(wslot[s][:, :, :], block_src(("We", e))).then_inc(w_loaded[s], 16)

            def load_tokens(k):
                s = k % 2
                sync.dma_start(zs[s][:, :], xs_dram[k * P:(k + 1) * P, :]).then_inc(xs_in[s], 16)

            def piece(w, x):
                name = x[0]
                block, used_up = block_of(x)
                if name == "load_hx":
                    if w.seg is SEG_FULL:
                        s, v = w.bank(("z", HALF - 1, NT - 1))
                        sync.wait_ge(bank_full[s], v)
                    elif w.seg is SEG_PRO:
                        sync.wait_ge(x_ready, w.p * ND)
                    sync.dma_start(hT[:, :, :], hidT[w.p].rearrange("(k p) t -> p k t", p=P)).then_inc(hidT_in, 16)
                elif name in ("load_hz", "load_hz_e"):
                    s, v = w.bank(("x", ND - 1) if name == "load_hz" else ("z", HALF - 1, NT - 1))
                    sync.wait_ge(bank_full[s], v)
                    sync.dma_start(hT[:, :, :], hidT[w.b].rearrange("(k p) t -> p k t", p=P)).then_inc(hidT_in, 16)
                elif name == "load_res":
                    sync.wait_ge(out_stored, w.e * (16 * NT) + 1)
                    sync.dma_start(res[:, :, :], hid[w.e].rearrange("(t p) c -> p t c", p=P)).then_inc(res_in, 16)
                elif x == ("xproj", 1):
                    s, v = w.bank(x)
                    sync.wait_ge(bank_taken[s], v)
                    sync.dma_start(b_dram[w.p], xdbl[RANK:RANK + NS, :]).then_inc(b_stored, 16)
                elif name == "store":
                    for t in range(NT):
                        sync.wait_ge(out_ready, w.d * NT + (t + 1))
                        sync.dma_start(out[w.d, tok(t), :], res[:, t, :]).then_inc(out_stored, 16)
                elif name == "load_E":
                    sync.wait_ge(owner_ready, w.e + 1)
                    sync.sem_inc(seen_sp, 1)
                    for k in range(2):
                        behind = W_X if w.seg is SEG_FULL else W_ZO
                        slot = w.weights(("We", k))[0]
                        s, v = w.bank(LAST_READER[behind[slot][-1]])
                        sync.wait_ge(bank_full[s], v)
                        load_expert(w, k)
                    sync.wait_ge(scattered, w.e * (16 * TOP * NT) + 16 * TOP * NT)
                    sync.sem_inc(seen_sp, 1)
                    for k in range(2):
                        s, v = w.bank(("yT", 1, NT - 2 + k))
                        sync.wait_ge(bank_full[s], v)
                        load_tokens(k)
                elif name == "xsT":
                    k = x[1]
                    if k + 2 < TILES:
                        s, v = w.bank(x)
                        sync.wait_ge(bank_full[s], v)
                        load_tokens(k + 2)
                elif used_up:
                    s, v = w.bank(x)
                    for after in w.seg.after[block]:
                        if after[0] != "We":
                            sync.wait_ge(bank_full[s], v)
                            slot = w.seg.place[block][0]
                            sync.dma_start(wslot[slot][:, :, :], block_src(after)).then_inc(w_loaded[slot], 16)
                        elif after[1] >= 2:
                            sync.wait_ge(bank_full[s], v)
                            load_expert(w, after[1])
                    if name == "moe":
                        k = x[1]
                        sync.wait_ge(bank_taken[s], v)
                        sync.dma_start(ys_dram[k * P:(k + 1) * P, :], ysb[k % 2]).then_inc(ys_stored[k % 2], 16)

            def period(w):
                for step, pieces in w.rows("sp"):
                    n, q = step // QUARTERS, step % QUARTERS
                    if w.seg.steps and q == 0:
                        if not (w.seg is SEG_PRO and n == 0):
                            sync.wait_ge(dbu_done, w.b * (NS * ND) + n * ND)
                        if n + 1 < NS:
                            load_B(w.b, n + 1)
                        elif w.seg is not SEG_EPI:
                            load_B(w.p, 0)
                    for x in pieces:
                        piece(w, x)
                if w.seg is SEG_FIRST:
                    sync.wait_ge(b_stored, 16)
                    load_B(w.p, 0)
                    sync.wait_ge(pads_ready, 4)
                    sync.dma_start(xs_dram.rearrange("(k p) c -> p k c", p=P), ysb[0].unsqueeze(1).broadcast_to((P, TILES, DM))).then_inc(xs_zeroed, 16)

            periods(sync, period, period, period)
            sync.wait_ge(out_stored, 16 * NT * NB + 1)

        @blk.tensor
        def _(pe):
            def accumulate(dst, lhs, rhs, n, share=None):
                for k in range(n) if share is None else range(n * share // 4, n * (share + 1) // 4):
                    mm = nc.tensor.matmul(dst, lhs(k), rhs(k), start=(k == 0), stop=(k == n - 1))
                return mm

            def state_part(G, n, i, first):
                g, t = i // NT, i % NT
                if t == 0:
                    pe.wait_ge(scan_done, G * ND + (g + 1) * KD)
                if not (first and n == 0 and i < 3):
                    pe.wait_ge(acc_done, G * NH + (i - 2 if i >= 3 else (-1, 0, -2)[i]))
                for j in range(KD):
                    mm = nc.tensor.transpose(hTp[i % 3][:, tok(j)], hst[n % 2][:, g * KD + j, tok(t)], ident[:, :])
                mm.then_inc(hT_done, 1)

            def piece(w, x, share):
                name = x[0]
                s, v = w.bank(x)
                ps = bank[s]
                if share == 0 and not (isinstance(v, int) and v == 1):
                    pe.wait_ge(bank_taken[s], v - 1)
                block, used_up = block_of(x)
                if block:
                    slot_w, loads = w.weights(block)
                    W = wslot[slot_w]
                    if share == 0:
                        pe.wait_ge(w_loaded[slot_w], loads * 16)
                if name == "x":
                    j = x[1]
                    if j == 0 and share == 0:
                        pe.wait_ge(hidT_in, 16 if w.seg is SEG_FIRST else w.p * 32)
                    mm = accumulate(ps[:, :], lambda k: W[:, k, tok(j % KD)], lambda k: hT[:, k, :], KD, share)
                elif name == "xproj":
                    c = slice(x[1] * (L // 2), (x[1] + 1) * (L // 2))
                    if share == 0:
                        if w.seg is SEG_FIRST:
                            pe.wait_ge(const_in, 16 * NCONST)
                            pe.wait_ge(pads_ready, 5)
                        pe.wait_ge(x_ready, w.p * ND + ND)
                    mm = accumulate(ps[0:KX, c], lambda k: w_x[:, k, :], lambda k: u[1 - w.odd][:, k, c], ND, share)
                elif name == "Ct":
                    sx, vx = w.bank(("xproj", 1))
                    pe.wait_ge(bank_taken[sx], vx)
                    for t in range(NT):
                        mm = nc.tensor.matmul(ps[:, t * NS:(t + 1) * NS], xdbl[0:KX, tok(t)], ident[0:KX, RANK + NS:KX], start=True, stop=True)
                elif name == "yinit":
                    j = x[1]
                    pe.wait_ge(xd_ready, w.p * ND + (j + 1))
                    for t in range(NT):
                        mm = nc.tensor.transpose(ps[:, tok(t)], third[j % 3][:, tok(t)], ident[:, :])
                elif name == "dt":
                    j = x[1]
                    mm = nc.tensor.matmul(ps[:, :], w_dt[:, j * P:(j + 1) * P], xdbl[0:RANK, :], start=True, stop=True)
                elif name == "z":
                    t = x[2]
                    if x[1] == 0 and t == 0 and share == 0:
                        pe.wait_ge(hidT_in, 2 * NB * 16 if w.seg is SEG_LAST else w.e * 32 + 48)
                    mm = accumulate(ps[:, :], lambda k: hT[:, k, tok(t)], lambda k: W[:, k, :], KD, share)
                elif name == "yT":
                    h, t = x[1], x[2]
                    pe.wait_ge(yg_done, w.e * (HALF * NT) + (h * NT + t + 1))
                    for k in range(KD):
                        mm = nc.tensor.transpose(ps[:, tok(k)], zy[t][:, tok(k)], ident[:, :])
                elif name == "out":
                    h, t = x[1], x[2]
                    sy, vy = w.bank(("yT", h, t))
                    if share == 0:
                        pe.wait_ge(bank_taken[sy], vy)
                    mm = accumulate(ps[:, :], lambda k: tokT[:, k, tok(t)], lambda k: W[:, k, :], KD, share)
                elif name == "x1T":
                    t = x[1]
                    pe.wait_ge(x1_ready, w.e * NT + (t + 1))
                    for k in range(KD):
                        mm = nc.tensor.transpose(ps[:, tok(k)], res[:, t, tok(k)], ident[:, :])
                elif name == "gate":
                    for t in (NT - 2, NT - 1):
                        sy, vy = w.bank(("x1T", t))
                        pe.wait_ge(bank_taken[sy], vy)
                    for t in range(NT):
                        mm = accumulate(ps[:, t * NE:(t + 1) * NE], lambda k: tokT[:, k, tok(t)], lambda k: gate[:, k, :], KD)
                elif name == "wT":
                    pe.wait_ge(wt_ready, w.e + 1)
                    for t in range(NT):
                        mm = nc.tensor.matmul(ps[0:NE, tok(t)], wt[:, t, :], ident[:, :], start=True, stop=True)
                elif name == "bias":
                    t = x[1]
                    sy, vy = w.bank(("wT",))
                    pe.wait_ge(bank_taken[sy], vy)
                    mm = nc.tensor.matmul(ps[:, :], wTs[:, tok(t)], expb, start=True, stop=True)
                elif name == "count":
                    pe.wait_ge(hits_ready, w.e + 1)
                    for t in range(NT):
                        mm = nc.tensor.matmul(ps[:, 0:NE], ones[:, :], hits[:, t, :], start=(t == 0), stop=(t == NT - 1))
                elif name == "rank":
                    for i in range(NT):
                        mm = nc.tensor.matmul(ps[:, i * NE:NT * NE], (ones if i else before)[:, :], hits[:, 0:NT - i, :],
                                              start=(i == 0), stop=(i == NT - 1))
                elif name == "xsT":
                    k = x[1]
                    slot, come, tiles_in = tile_slot(k)
                    pe.wait_ge(xs_in[slot], w.e * (16 * tiles_in) + 16 * come)
                    for i in range(KD):
                        mm = nc.tensor.transpose(ps[:, tok(i)], zs[slot][:, tok(i)], ident[:, :])
                elif name == "moe":
                    k = x[1]
                    sx, vx = w.bank(("xsT", k))
                    if share == 0:
                        pe.wait_ge(bank_taken[sx], vx)
                    mm = accumulate(ps[:, :], lambda i: tokT[:, i, tok(k % NT)], lambda i: W[:, i, :], KD, share)
                if share == SHARES.get(name, 1) - 1:
                    mm.then_inc(bank_full[s], 1)

            def period(w):
                first = w.seg is SEG_PRO
                for step, pieces in w.rows("pe"):
                    n, q = step // QUARTERS, step % QUARTERS
                    m = n if q == 3 else n - 1
                    parts = (2 * ((q + 1) % QUARTERS), 2 * ((q + 1) % QUARTERS) + 1)
                    if not w.seg.steps or (first and m < 0):
                        parts = ()
                    for i in parts[:1]:
                        state_part(w.b * NS + m, m % NS, i, first)
                    for x, share in pieces:
                        piece(w, x, share)
                    for i in parts[1:]:
                        state_part(w.b * NS + m, m % NS, i, first)

            def last(w):
                for i in range(2, NH):
                    state_part(NB * NS - 1, NS - 1, i, False)
                period(w)

            periods(pe, period, last, lambda w: None)

        @blk.scalar
        def _(act):
            nc.scalar.preload_act_table_set("natural_log_exp_and_others")
            act.wait_ge(conv_in, 32)

            def rsqrt(e, base):
                act.wait_ge(mv_ready, e * (2 * NT) + (base + 1) * NT)
                nc.scalar.activation(lnv[:, :], mv[:, :, 1], ACT.Ln, bias=eps[:, 0:1]).then_inc(lnv_ready, 1)
                act.wait_ge(lnv_ready, e * 2 + (base + 1))
                nc.scalar.activation(rstd[:, :], lnv[:, :], ACT.Exp, scale=-0.5).then_inc(rstd_ready, 1)

            def piece(w, x):
                name = x[0]
                if w.seg is SEG_FIRST and name in ("skip", "yinit"):
                    return
                if w.seg is SEG_FIRST and x == ("xproj", 0):
                    act.wait_ge(const_in, 16 * NCONST)
                    act.wait_ge(pads_ready, 3)
                    nc.scalar.activation(negA[:, :, :], negA[:, :, :], ACT.Exp).then_inc(negA_ready, 1)
                if name in ("x", "xproj", "yinit", "dt", "z", "yT", "x1T", "wT", "xsT", "moe"):
                    s, v = w.bank(x)
                    ps = bank[s]
                    act.wait_ge(bank_full[s], v)
                if name == "x":
                    j = x[1]
                    if not (w.seg is SEG_FIRST and j < 2):
                        act.wait_ge(conv_done, w.p * ND + (j - 1))
                    nc.scalar.activation(u[1 - w.odd][:, j, :], ps[:, :], ACT.Identity, bias=cb[:, j:j + 1], scale=cw[:, j, TAPS - 1:TAPS])
                    nc.scalar.activation(xpre[j % 2][:, TAPS - 1:], ps[:, :], ACT.Copy).then_inc(bank_taken[s], 1)
                elif name == "sig":
                    j, base = x[1], w.p * (3 * ND) + 3 * x[1]
                    a = side[j % 2][:, :]
                    if not (w.seg is SEG_FIRST and j < 2):
                        act.wait_ge(x_ready, w.p * ND + (j - 1))
                    act.wait_ge(conv_done, w.p * ND + (j + 1))
                    nc.scalar.activation(a, u[1 - w.odd][:, j, :], ACT.Exp, scale=-1.0).then_inc(sig_step, 1)
                    act.wait_ge(sig_step, base + 1)
                    nc.scalar.activation(a, a, ACT.Ln, bias=1.0).then_inc(sig_step, 1)
                    act.wait_ge(sig_step, base + 2)
                    nc.scalar.activation(a, a, ACT.Exp, scale=-1.0).then_inc(sig_step, 1)
                elif name == "xproj":
                    c = slice(x[1] * (L // 2), (x[1] + 1) * (L // 2))
                    if not (isinstance(w.p, int) and w.p == 0):
                        act.wait_ge(b_stored, w.p * 16)
                    nc.scalar.activation(xdbl[:, c], ps[0:KX, c], ACT.Copy).then_inc(bank_taken[s], 1)
                elif name == "yinit":
                    j = x[1]
                    if w.seg is SEG_FULL:
                        act.wait_ge(yg_done, w.e * (HALF * NT) + HALF * NT)
                    nc.scalar.activation(y[1 - w.odd][:, :, j * P:(j + 1) * P], ps[:, :].rearrange("p (t d) -> p t d", t=NT),
                                         ACT.Copy).then_inc(bank_taken[s], 1)
                elif name == "skip":
                    j = x[1]
                    act.wait_ge(x_ready, w.p * ND + ND)
                    if j > 2:
                        sy, vy = w.bank(("yinit", j - 3))
                        act.wait_ge(bank_full[sy], vy)
                    nc.scalar.activation(third[j % 3], u[1 - w.odd][:, j, :], ACT.Copy, scale=dskip[:, j:j + 1]).then_inc(xd_ready, 1)
                elif name == "dt":
                    j, a = x[1], third[x[1] % 3]
                    if not (w.seg is SEG_FIRST and j < 3):
                        act.wait_ge(delta_ready, w.p * ND + (j - 2))
                    nc.scalar.activation(a, ps[:, :], ACT.Abs, bias=dtb[:, j:j + 1]).then_inc(sp_step, 1)
                    nc.scalar.activation(delta[1 - w.odd][:, j, :], ps[:, :], ACT.Relu, bias=dtb[:, j:j + 1]).then_inc(bank_taken[s], 1)
                    act.wait_ge(sp_step, w.p * (2 * ND) + (2 * j + 1))
                    nc.scalar.activation(a, a, ACT.Exp, scale=-1.0).then_inc(sp_step, 1)
                    act.wait_ge(sp_step, w.p * (2 * ND) + (2 * j + 2))
                    nc.scalar.activation(a, a, ACT.Ln, bias=1.0).then_inc(sp_ready, 1)
                elif name == "z":
                    i = x[1] * NT + x[2]
                    if i == 0:
                        act.wait_ge(combined, w.e * (TOP * NT) + 1)
                    if i > 1:
                        act.wait_ge(yg_done, w.e * (HALF * NT) + (i - 1))
                    base = w.e * (2 * HALF * NT) + 2 * i
                    a = side[i % 2][:, :]
                    nc.scalar.activation(zy[i % Z_SLOTS], ps[:, :], ACT.Copy)
                    nc.scalar.activation(a, ps[:, :], ACT.Exp, scale=-1.0).then_inc(bank_taken[s], 1)
                    act.wait_ge(bank_taken[s], v)
                    nc.scalar.activation(a, a, ACT.Ln, bias=1.0).then_inc(zsig_step, 1)
                    act.wait_ge(zsig_step, base + 1)
                    nc.scalar.activation(a, a, ACT.Exp, scale=-1.0).then_inc(zsig_step, 1)
                elif name in ("yT", "x1T", "xsT"):
                    t = x[-1] % NT
                    nc.scalar.activation(tokT[:, :, tok(t)], ps[:, :].rearrange("p (k t) -> p k t", k=KD), ACT.Copy).then_inc(bank_taken[s], 1)
                elif name == "ln1":
                    rsqrt(w.e, 0)
                elif name == "ln2":
                    rsqrt(w.d, 1)
                elif name == "gate":
                    act.wait_ge(gap_ready, w.e + 1)
                    nc.scalar.activation(eg[:, :], gap[:, :], ACT.Exp).then_inc(eg_ready, 1)
                elif name == "moe":
                    slot, come, tiles_in = tile_slot(x[1])
                    if come > 1:
                        act.wait_ge(ys_stored[slot], w.e * (16 * tiles_in) + 16 * (come - 1))
                    nc.scalar.activation(ysb[slot], ps[:, :], ACT.Copy).then_inc(bank_taken[s], 1)
                elif name == "wT":
                    nc.scalar.activation(wTs, ps[0:NE, :], ACT.Copy).then_inc(bank_taken[s], 1)

            def period(w):
                if w.seg is SEG_PRO:
                    act.wait_ge(negA_ready, 2)
                for step, pieces in w.rows("act"):
                    n, q = step // QUARTERS, step % QUARTERS
                    if w.seg.steps:
                        for j in (2 * q, 2 * q + 1):
                            if n == 0:
                                act.wait_ge(u_ready, w.b * ND + (j + 1))
                            if not (w.seg is SEG_PRO and n == 0 and j < 2):
                                act.wait_ge(scan_done, w.b * (NS * ND) + (n * ND + j - 1))
                            nc.scalar.activation(dA[j % 2][:, :], delta[w.odd][:, j, :], ACT.Exp, scale=negA[:, j, n:n + 1]).then_inc(exp_done, 1)
                    for x in pieces:
                        piece(w, x)

            periods(act, period, period, period)

        @blk.gpsimd
        def _(pool):
            def piece(w, x):
                if x[0] == "scatter":
                    t = x[1]
                    if t == 0:
                        pool.wait_ge(place_ready, w.e + 1)
                        pool.sem_inc(seen_pool, 1)
                    for c in range(TOP):
                        nc.gpsimd.indirect_dma_start(xs_dram[:, :], bass.IndirectOffsetOnAxis(ap=place[:, t, c:c + 1], axis=0),
                                                     res[:, t, :], None).then_inc(scattered, 16)
                elif x[0] == "gather":
                    t = x[1]
                    if t == 0:
                        for k in range(2):
                            slot, _, tiles_in = tile_slot(k)
                            pool.wait_ge(ys_stored[slot], w.e * (16 * tiles_in) + 16 * tiles_in)
                            pool.sem_inc(seen_pool, 1)
                    for c in range(TOP):
                        nc.gpsimd.indirect_dma_start(choices(t)[c], None, ys_dram[:, :],
                                                     bass.IndirectOffsetOnAxis(ap=place[:, t, c:c + 1], axis=0)).then_inc(gathered[t // 2], 16)
                elif x[0] == "sig":
                    j, x_j = x[1], u[1 - w.odd][:, x[1], :]
                    pool.wait_ge(sig_step, w.p * (3 * ND) + 3 * (j + 1))
                    nc.gpsimd.tensor_tensor(x_j, x_j, side[j % 2][:, :], ALU.mult).then_inc(x_ready, 1)
                elif x[0] == "dt":
                    delta_of(w, x[1])

            def delta_of(w, j):
                d, x_j = delta[1 - w.odd][:, j, :], u[1 - w.odd][:, j, :]
                pool.wait_ge(sp_ready, w.p * ND + (j + 1))
                if w.seg is not SEG_FIRST:
                    nc.gpsimd.tensor_tensor(d, d, third[j % 3], ALU.add).then_inc(delta_ready, 1)
                pool.wait_ge(delta_ready, w.p * ND + (j + 1))
                nc.gpsimd.tensor_tensor(x_j, d, x_j, ALU.mult).then_inc(u_ready, 1)

            def period(w):
                for step, pieces in w.rows("pool"):
                    n, q = step // QUARTERS, step % QUARTERS
                    if w.seg.steps:
                        if q == 0:
                            pool.wait_ge(b_loaded[n % 2], w.b * (16 * NS // 2) + 16 * (n // 2 + 1))
                        for j in (2 * q, 2 * q + 1):
                            if n == 0:
                                pool.wait_ge(u_ready, w.b * ND + (j + 1))
                            if not (w.seg is SEG_PRO and n == 0 and j < 4):
                                pool.wait_ge(scan_done, w.b * (NS * ND) + (n * ND + j - 3))
                            nc.gpsimd.tensor_tensor(dbu[j % 4][:, :], u[w.odd][:, j, :], Bbc[n % 2][:, :], ALU.mult).then_inc(dbu_done, 1)
                    for x in pieces:
                        piece(w, x)
                if w.seg is SEG_PRO:
                    pool.wait_ge(xs_zeroed, 16)

            periods(pool, period, period, period)

        @blk.vector
        def _(dve):
            for s in range(2):
                nc.vector.memset(xpre[s][:, 0:TAPS - 1], 0.0).then_inc(pads_ready, 1)
            dve.sem_inc(combined, 1)
            nc.vector.memset(eps[:, :], EPS).then_inc(pads_ready, 1)
            nc.vector.memset(ysb[0], 0.0).then_inc(pads_ready, 1)
            nc.vector.memset(ones[:, :], 1.0).then_inc(pads_ready, 1)
            dve.wait_ge(pads_ready, 5)

            def state_part(G, n, i, odd, first):
                g, t = i // NT, i % NT
                y_part = y[odd][:, t, g * DM:(g + 1) * DM]
                dve.wait_ge(hT_done, G * NH + (i + 1))
                if not (first and n == 0):
                    dve.wait_ge(acc_done, G * NH + (i + 1 - NH))
                nc.vector.scalar_tensor_tensor(y_part, hTp[i % 3][:, :], Ct[odd][:, t, n:n + 1], y_part, ALU.mult, ALU.add).then_inc(acc_done, 1)

            ROUTE_STEPS = 2 * NT + 12

            def norm(e, base, t):
                dve.wait_ge(rstd_ready, e * 2 + (base + 1))
                return nc.vector.tensor_scalar(res[:, t, :], res[:, t, :], mv[:, t, 0:1], rstd[:, t:t + 1], ALU.subtract, ALU.mult)

            def stats(t):
                nc.vector.bn_stats(st[:, t, :], res[:, t, :]).then_inc(st_done, 1)

            def aggregate(e, base):
                for t in range(NT):
                    dve.wait_ge(st_done, e * (2 * NT) + (base * NT + t + 1))
                    dve.sem_inc(seen, 1)
                    nc.vector.bn_aggr(mv[:, t, :], st[:, t, :]).then_inc(mv_ready, 1)

            def piece(w, x):
                name = x[0]
                if name in ("Ct", "out", "gate", "bias"):
                    s, v = w.bank(x)
                    ps = bank[s]
                    dve.wait_ge(bank_full[s], v)
                if name == "x":
                    j = x[1]
                    s, v = w.bank(x)
                    dve.wait_ge(bank_taken[s], v)
                    for k in range(TAPS - 1):
                        if k:
                            dve.wait_ge(tap_done, w.p * (2 * ND) + (2 * j + k))
                        x_j = u[1 - w.odd][:, j, :]
                        tap = nc.vector.scalar_tensor_tensor(x_j, xpre[j % 2][:, k:k + L], cw[:, j, k:k + 1], x_j, ALU.mult, ALU.add)
                        tap.then_inc(conv_done if k == TAPS - 2 else tap_done, 1)
                elif name == "skip" and w.seg is SEG_FIRST:
                    j = x[1]
                    dve.wait_ge(const_in, 16 * NCONST)
                    dve.wait_ge(x_ready, w.p * ND + ND)
                    if j > 2:
                        sy, vy = w.bank(("yinit", j - 3))
                        dve.wait_ge(bank_full[sy], vy)
                    nc.vector.tensor_scalar(third[j % 3], u[1 - w.odd][:, j, :], dskip[:, j:j + 1], None, ALU.mult).then_inc(xd_ready, 1)
                elif name == "yinit" and w.seg is SEG_FIRST:
                    j = x[1]
                    s, v = w.bank(x)
                    dve.wait_ge(bank_full[s], v)
                    nc.vector.tensor_copy(y[1 - w.odd][:, :, j * P:(j + 1) * P], bank[s][:, :].rearrange("p (t d) -> p t d", t=NT)).then_inc(bank_taken[s], 1)
                elif name == "dt" and w.seg is SEG_FIRST:
                    j, d = x[1], delta[1 - w.odd][:, x[1], :]
                    dve.wait_ge(sp_ready, w.p * ND + (j + 1))
                    nc.vector.tensor_tensor(d, d, third[j % 3], ALU.add).then_inc(delta_ready, 1)
                elif name == "Ct":
                    if w.seg is SEG_FIRST:
                        dve.wait_ge(negA_ready, 1)
                        nc.vector.tensor_scalar(negA[:, :, :], negA[:, :, :], -1.0, None, ALU.mult).then_inc(negA_ready, 1)
                    nc.vector.tensor_copy(Ct[1 - w.odd][:, :, :], ps[:, 0:NT * NS].rearrange("p (t n) -> p t n", t=NT)).then_inc(bank_taken[s], 1)
                elif name == "z":
                    h, t = x[1], x[2]
                    i = w.e * (HALF * NT) + (h * NT + t)
                    s, v = w.bank(x)
                    dve.wait_ge(bank_taken[s], v)
                    dve.wait_ge(acc_done, w.e * (NS * NH) + ((NS - 1) * NH + h * NT + t + 1))
                    nc.vector.tensor_tensor(zy[t], zy[t], y[1 - w.odd][:, t, h * DM:(h + 1) * DM], ALU.mult).then_inc(zy_done, 1)
                    dve.wait_ge(zy_done, i + 1)
                    dve.wait_ge(zsig_step, i * 2 + 2)
                    nc.vector.tensor_tensor(zy[t], zy[t], side[t % 2][:, :], ALU.mult).then_inc(yg_done, 1)
                elif name == "out":
                    h, t = x[1], x[2]
                    if h == 0 and t == 0:
                        dve.wait_ge(res_in, w.e * 16 + 16)
                    if h:
                        so, vo = w.bank(("out", 0, t))
                        dve.wait_ge(bank_taken[so], vo)
                    nc.vector.tensor_tensor(res[:, t, :], ps[:, :], res[:, t, :], ALU.add).then_inc(bank_taken[s], 1)
                    if h:
                        dve.wait_ge(bank_taken[s], v)
                        stats(t)
                elif name == "ln1":
                    aggregate(w.e, 0)
                elif name == "ln1x":
                    for t in range(NT):
                        norm(w.e, 0, t).then_inc(x1_ready, 1)
                elif name == "gate":
                    base = w.e * ROUTE_STEPS
                    nc.vector.tensor_copy(lg[:, :, :], ps[:, 0:NT * NE].rearrange("p (t e) -> p t e", t=NT)).then_inc(bank_taken[s], 1)
                    dve.wait_ge(bank_taken[s], v)
                    dve.sem_inc(seen, 1)
                    for t in range(NT):
                        nc.vector.max(mx[:, t, :], lg[:, t, :]).then_inc(route_step, 1)
                    for t in range(NT):
                        dve.wait_ge(route_step, base + (t + 1))
                        dve.sem_inc(seen, 1)
                        nc.vector.max_index(mi[:, t, :], mx[:, t, :], lg[:, t, :]).then_inc(route_step, 1)
                    nc.vector.tensor_tensor(gap[:, :], mx[:, :, 1], mx[:, :, 0], ALU.subtract).then_inc(gap_ready, 1)
                    dve.wait_ge(route_step, base + 2 * NT)
                    nc.vector.tensor_copy(pick[:, :, :], mi[:, :, 0:TOP]).then_inc(route_step, 1)
                    dve.wait_ge(route_step, base + (2 * NT + 1))
                    nc.vector.tensor_tensor(hit[:, :, :, :], ramp[:, 0:NE].unsqueeze(1).unsqueeze(1).broadcast_to((P, NT, TOP, NE)),
                                            pick[:, :, :].unsqueeze(3).broadcast_to((P, NT, TOP, NE)), ALU.is_equal).then_inc(route_step, 1)
                    dve.wait_ge(route_step, base + (2 * NT + 2))
                    nc.vector.tensor_tensor(hits[:, :, :], hit[:, :, 0, :], hit[:, :, 1, :], ALU.add).then_inc(hits_ready, 1)
                elif name == "place":
                    base = w.e * ROUTE_STEPS + (2 * NT + 2)
                    sc, vc = w.bank(("count",))
                    dve.wait_ge(bank_full[sc], vc)
                    nc.vector.tensor_tensor(over[:, :, :], bank[sc][:, 0:NE].unsqueeze(2).broadcast_to((P, NE, NT)),
                                            ramp[:, 2 * NE:2 * NE + NT].unsqueeze(1).broadcast_to((P, NE, NT)), ALU.is_gt).then_inc(bank_taken[sc], 1)
                    dve.wait_ge(bank_taken[sc], vc)
                    nc.vector.tensor_reduce(tiles[:, :], over[:, :, :], AX.X, ALU.add).then_inc(route_step, 1)
                    dve.wait_ge(route_step, base + 1)
                    nc.vector.tensor_tensor_scan(end[:, :], ones[:, 0:NE], tiles[:, :], 0.0, ALU.mult, ALU.add).then_inc(route_step, 1)
                    dve.wait_ge(route_step, base + 2)
                    nc.vector.tensor_tensor(begin[:, :], end[:, :], tiles[:, :], ALU.subtract).then_inc(route_step, 1)
                    nc.vector.tensor_tensor(past[:, :, :], ramp[0:1, 0:TILES].unsqueeze(2).broadcast_to((1, TILES, NE)),
                                            end[0:1, :].unsqueeze(1).broadcast_to((1, TILES, NE)), ALU.is_ge).then_inc(route_step, 1)
                    sr, vr = w.bank(("rank",))
                    dve.wait_ge(bank_full[sr], vr)
                    dve.wait_ge(route_step, base + 3)
                    nc.vector.scalar_tensor_tensor(row[:, :, :], begin[:, :].unsqueeze(1).broadcast_to((P, NT, NE)), float(P),
                                                   bank[sr][:, 0:NT * NE].rearrange("p (t e) -> p t e", t=NT), ALU.mult, ALU.add).then_inc(bank_taken[sr], 1)
                    dve.wait_ge(route_step, base + 4)
                    nc.vector.tensor_reduce(owner[:, :], past[:, :, :], AX.X, ALU.add).then_inc(route_step, 1)
                    dve.wait_ge(bank_taken[sr], vr)
                    nc.vector.tensor_tensor(hit_row[:, :, :, :], hit[:, :, :, :], row[:, :, :].unsqueeze(2).broadcast_to((P, NT, TOP, NE)),
                                            ALU.mult).then_inc(route_step, 1)
                    dve.wait_ge(route_step, base + 5)
                    nc.vector.tensor_scalar(tile_expert[:, :], owner[:, :], float(NE - 1), None, ALU.min).then_inc(owner_ready, 1)
                    dve.wait_ge(route_step, base + 6)
                    with nc.allow_low_precision(reason="whole numbers below 2 ** 24"):
                        nc.vector.tensor_reduce(place[:, :, :], hit_row[:, :, :, :], AX.X, ALU.add).then_inc(place_ready, 1)
                elif name == "route":
                    base = w.e * ROUTE_STEPS + (2 * NT + 8)
                    dve.wait_ge(eg_ready, w.e + 1)
                    nc.vector.tensor_scalar(den[:, :], eg[:, :], 1.0, None, ALU.add).then_inc(route_step, 1)
                    dve.wait_ge(route_step, base + 1)
                    nc.vector.reciprocal(mix[:, :, 0], den[:, :]).then_inc(route_step, 1)
                    dve.wait_ge(route_step, base + 2)
                    nc.vector.tensor_tensor(mix[:, :, 1], eg[:, :], mix[:, :, 0], ALU.mult).then_inc(route_step, 1)
                    dve.wait_ge(route_step, base + 3)
                    nc.vector.tensor_tensor(hit_w[:, :, :, :], hit[:, :, :, :], mix[:, :, :].unsqueeze(3).broadcast_to((P, NT, TOP, NE)),
                                            ALU.mult).then_inc(route_step, 1)
                    dve.wait_ge(route_step, base + 4)
                    nc.vector.tensor_tensor(wt[:, :, :], hit_w[:, :, 0, :], hit_w[:, :, 1, :], ALU.add).then_inc(wt_ready, 1)
                elif name == "bias":
                    t = x[1]
                    dve.wait_ge(scattered, w.e * (16 * TOP * NT) + 16 * TOP * NT)
                    nc.vector.tensor_tensor(res[:, t, :], ps[:, :], res[:, t, :], ALU.add).then_inc(bank_taken[s], 1)
                elif x == ("gather", 0):
                    for s, v in dict(w.bank(("bias", t)) for t in range(NT)).items():
                        dve.wait_ge(bank_taken[s], v)
                elif name == "combine":
                    t = x[1]
                    dve.wait_ge(gathered[t // 2], w.d * (16 * TOP * 2) + 16 * TOP * 2)
                    for c in range(TOP):
                        if c:
                            dve.wait_ge(combined, w.d * (TOP * NT) + (TOP * t + c + 1))
                        nc.vector.scalar_tensor_tensor(res[:, t, :], choices(t)[c], mix[:, t, c:c + 1], res[:, t, :],
                                                       ALU.mult, ALU.add).then_inc(combined, 1)
                    dve.wait_ge(combined, w.d * (TOP * NT) + (TOP * (t + 1) + 1))
                    stats(t)
                elif name == "ln2":
                    aggregate(w.d, 1)
                elif name == "ln2x":
                    for t in range(NT):
                        norm(w.d, 1, t).then_inc(out_ready, 1)

            def period(w):
                first = w.seg is SEG_PRO
                for step, pieces in w.rows("dve"):
                    n, q = step // QUARTERS, step % QUARTERS
                    done = n * NH + 2 * q - (NH - 1)

                    def add_part(k):
                        if w.seg.steps and not (first and k < 0):
                            state_part(w.b * NS + k // NH, k // NH % NS, k % NH, w.odd if k >= 0 else 1 - w.odd, first)

                    add_part(done)
                    for j in (2 * q, 2 * q + 1) if w.seg.steps else ():
                        tile = n * ND + j + 1
                        dve.wait_ge(exp_done, w.b * (NS * ND) + tile)
                        dve.wait_ge(dbu_done, w.b * (NS * ND) + tile)
                        if not (first and n < 2):
                            dve.wait_ge(hT_done, w.b * (NS * NH) + ((n - 2) * NH + (j // KD + 1) * NT))
                        nc.vector.tensor_tensor_scan(hst[n % 2][:, j, :], dA[j % 2][:, :], dbu[j % 4][:, :], 0.0, ALU.mult, ALU.add).then_inc(scan_done, 1)
                    add_part(done + 1)
                    for x in pieces:
                        piece(w, x)

            def last(w):
                for i in range(1, NH):
                    state_part(NB * NS - 1, NS - 1, i, 1, False)
                period(w)

            periods(dve, period, last, period)


def kernel(**inputs):
    import numpy as np
    import concourse.bacc as bacc
    from concourse.bass_utils import run_bass_kernel_spmd

    def arr(name):
        return np.asarray(inputs[name])

    hid = arr("L0_attn_hidden_states")
    arrays = {
        "hid": hid,
        "hidT": hid.transpose(0, 2, 1),
        "w_inT": arr("L0_attn_in_proj_w").T,
        "conv_w": arr("L0_attn_conv_w"),
        "conv_b": arr("L0_attn_conv_b"),
        "w_xT": arr("L0_attn_x_proj_w").T,
        "w_dtT": arr("L0_attn_dt_proj_w").T,
        "dt_b": arr("L0_attn_dt_proj_b"),
        "A_log": arr("L0_attn_A_log"),
        "D": arr("L0_attn_D"),
        "w_outT": arr("L0_attn_out_proj_w").T,
        "gateT": arr("L0_ffn_gate_w").T,
        "w_expT": arr("L0_ffn_expert_w").transpose(0, 2, 1),
        "exp_b": arr("L0_ffn_expert_b"),
        "ident_c": np.eye(P, dtype=np.float32),
        "before_c": np.triu(np.ones((P, P), np.float32), 1),
        "ramp_c": np.tile(np.concatenate([np.arange(2 * NE), P * np.arange(NT)]).astype(np.float32), (P, 1)),
    }
    arrays = {k: np.ascontiguousarray(v) for k, v in arrays.items()}
    nc = bacc.Bacc("TRN2", target_bir_lowering=False, num_devices=1)
    args = [nc.dram_tensor(f"in_{k}", v.shape, mybir.dt.from_np(v.dtype), kind="ExternalInput").ap() for k, v in arrays.items()]
    out = nc.dram_tensor("out", hid.shape, F32, kind="ExternalOutput").ap()
    build(nc, *args, out)
    r = run_bass_kernel_spmd(nc, [{f"in_{k}": v for k, v in arrays.items()}], core_ids=[0])
    return r.results[0]["out"]
```
